# Optimizing a Trainium2 kernel written in Bass

```python
import numpy as np
import jax
import jax.numpy as jnp

def _softmax(x, axis=-1):
    return jax.nn.softmax(x, axis=axis)

def _gelu(x):
    return jax.nn.gelu(x, approximate=True)

def _silu(x):
    return jax.nn.silu(x)

def _sigmoid(x):
    return jax.nn.sigmoid(x)

def _layernorm(x, axis=-1, eps=1e-05):
    m = jnp.mean(x, axis=axis, keepdims=True)
    v = jnp.var(x, axis=axis, keepdims=True)
    return (x - m) / jnp.sqrt(v + eps)

def _scatter_add(tgt, idx, src, axis=0):
    return tgt.at[idx].add(src)

def _segment_sum(src, seg, n):
    return jax.ops.segment_sum(src, seg, n)
kernel_name = 'mk_conv_preact_d4_conv_nchw256_r2_007c32'

def setup_inputs(seed: int=0):
    np.random.seed(seed)
    _w = jnp.asarray

    def _rec_inputs():
        import jax
        import jax.numpy as jnp
        _gk = jax.random.key(seed)
        x = -0.0001732 + 1 * jax.random.normal(jax.random.fold_in(_gk, 1), (2, 128, 48, 48), jnp.float32)
        return x
    x = _rec_inputs()

    def _L0_conv_setup():
        import jax, jax.numpy as jnp
        import numpy as np
        K = 3
        PAD = 1
        STRIDE = 1
        DIL = 1

        def _bilinear_gather(feat, y, x):
            B, C, H, W = feat.shape
            feat_flat = feat.reshape(B, C, H * W)
            y0 = jnp.floor(y)
            x0 = jnp.floor(x)
            out = jnp.zeros((B, C) + y.shape[1:], feat.dtype)
            for yi in (y0, y0 + 1.0):
                for xi in (x0, x0 + 1.0):
                    wgt = (1.0 - jnp.abs(y - yi)) * (1.0 - jnp.abs(x - xi))
                    valid = (yi >= 0) & (yi <= H - 1) & (xi >= 0) & (xi <= W - 1)
                    yc = jnp.clip(yi, 0, H - 1).astype(jnp.int32)
                    xc = jnp.clip(xi, 0, W - 1).astype(jnp.int32)
                    idx = (yc * W + xc).reshape(B, 1, -1)
                    g = jnp.take_along_axis(feat_flat, idx, axis=2).reshape(B, C, *y.shape[1:])
                    out = out + g * (wgt * valid)[:, None]
            return out
        key = jax.random.key(seed)
        k1, k2, k3, k4, k5 = jax.random.split(key, 5)
        B, Cin, Cout, H, W = (2, 128, 128, 48, 48)
        x = jax.random.normal(k1, (B, Cin, H, W), jnp.float32)
        pw_w = jax.random.normal(k2, (Cout, Cin), jnp.float32) / np.sqrt(Cin)
        off_w = jax.random.normal(k3, (2 * K * K, Cout), jnp.float32) * 0.01
        off_b = jax.random.normal(k4, (2 * K * K,), jnp.float32) * 0.5
        dw_w = jax.random.normal(k5, (Cout, K, K), jnp.float32) / K
        return {'x': x, 'pw_w': pw_w, 'off_w': off_w, 'off_b': off_b, 'dw_w': dw_w}
    _L0_conv_all = _L0_conv_setup()
    _L0_conv_in = {k: v for k, v in _L0_conv_all.items() if k in ('pw_w', 'off_w', 'off_b', 'dw_w')}
    del _L0_conv_all

    def _L1_conv_setup():
        import jax, jax.numpy as jnp
        import numpy as np
        C = 128
        K = 7
        PAD = (K - 1) // 2
        RED = 4
        EPS = 1e-05
        key = jax.random.key(seed)
        k0, k1, k2 = jax.random.split(key, 3)
        B, H, W = (4, 56, 56)
        x = jax.random.normal(k0, (B, C, H, W), jnp.float32)
        w1 = jax.random.normal(k1, (C // RED, C), jnp.float32) * 0.05
        b1 = jnp.zeros((C // RED,), jnp.float32)
        gamma = jnp.ones((C // RED,), jnp.float32)
        beta = jnp.zeros((C // RED,), jnp.float32)
        w2 = jax.random.normal(k2, (K * K * C, C // RED), jnp.float32) * 0.05
        b2 = jnp.zeros((K * K * C,), jnp.float32)
        return dict(x=x, w1=w1, b1=b1, gamma=gamma, beta=beta, w2=w2, b2=b2)
    _L1_conv_all = _L1_conv_setup()
    _L1_conv_in = {k: v for k, v in _L1_conv_all.items() if k in ('w1', 'b1', 'gamma', 'beta', 'w2', 'b2')}
    del _L1_conv_all

    def _L2_conv_setup():
        import jax, jax.numpy as jnp
        import numpy as np
        KH, KW = (3, 3)
        K = KH * KW
        PAD, STRIDE, DIL = (1, 1, 1)

        def _conv(x, w, b):
            y = jax.lax.conv_general_dilated(x, w, (STRIDE, STRIDE), ((PAD, PAD), (PAD, PAD)), rhs_dilation=(DIL, DIL), dimension_numbers=('NCHW', 'OIHW', 'NCHW'))
            return y + b[None, :, None, None]

        def _bilinear_gather(x, py, px):
            B, C, H, W = x.shape
            y0 = jnp.floor(py)
            x0 = jnp.floor(px)
            wy1 = py - y0
            wx1 = px - x0
            wy0 = 1.0 - wy1
            wx0 = 1.0 - wx1
            xf = x.reshape(B, C, H * W)

            def g(yi, xi):
                valid = (yi >= 0) & (yi < H) & (xi >= 0) & (xi < W)
                yc = jnp.clip(yi, 0, H - 1).astype(jnp.int32)
                xc = jnp.clip(xi, 0, W - 1).astype(jnp.int32)
                idx = (yc * W + xc).reshape(B, -1)
                v = jax.vmap(lambda im, ix: im[:, ix])(xf, idx)
                v = v.reshape(B, C, *yi.shape[1:])
                return v * valid[:, None].astype(x.dtype)
            return (wy0 * wx0)[:, None] * g(y0, x0) + (wy0 * wx1)[:, None] * g(y0, x0 + 1) + (wy1 * wx0)[:, None] * g(y0 + 1, x0) + (wy1 * wx1)[:, None] * g(y0 + 1, x0 + 1)
        key = jax.random.key(seed)
        k1, k2, k3 = jax.random.split(key, 3)
        B, C, H, W = (8, 128, 32, 32)
        x = jax.random.normal(k1, (B, C, H, W), dtype=jnp.float32)
        w_om = jax.random.normal(k2, (3 * K, C, KH, KW), dtype=jnp.float32) * 0.01
        b_om = jnp.zeros((3 * K,), dtype=jnp.float32)
        w_dc = jax.random.normal(k3, (C, C, KH, KW), dtype=jnp.float32) * (1.0 / np.sqrt(C * K))
        b_dc = jnp.zeros((C,), dtype=jnp.float32)
        return {'x': x, 'w_om': w_om, 'b_om': b_om, 'w_dc': w_dc, 'b_dc': b_dc}
    _L2_conv_all = _L2_conv_setup()
    _L2_conv_in = {k: v for k, v in _L2_conv_all.items() if k in ('w_om', 'b_om', 'w_dc', 'b_dc')}
    del _L2_conv_all

    def _L3_conv_setup():
        import jax, jax.numpy as jnp
        import numpy as np
        CHANNEL = 128
        NUM_HEADS = 8
        HEAD_DIM = CHANNEL // NUM_HEADS
        key = jax.random.key(seed)
        k0, k1, k2, k3, k4 = jax.random.split(key, 5)
        s = 1.0 / np.sqrt(CHANNEL)
        return {'x': jax.random.normal(k0, (16, CHANNEL, 32, 32), dtype=jnp.float32), 'Wq': jax.random.uniform(k1, (CHANNEL, CHANNEL), jnp.float32, -s, s), 'Wk': jax.random.uniform(k2, (CHANNEL, CHANNEL), jnp.float32, -s, s), 'Wv': jax.random.uniform(k3, (CHANNEL, CHANNEL), jnp.float32, -s, s), 'Wo': jax.random.uniform(k4, (CHANNEL, CHANNEL), jnp.float32, -s, s)}
    _L3_conv_all = _L3_conv_setup()
    _L3_conv_in = {k: v for k, v in _L3_conv_all.items() if k in ('Wq', 'Wk', 'Wv', 'Wo')}
    del _L3_conv_all
    return {'x': x, 'L0_conv_pw_w': _L0_conv_in['pw_w'], 'L0_conv_off_w': _L0_conv_in['off_w'], 'L0_conv_off_b': _L0_conv_in['off_b'], 'L0_conv_dw_w': _L0_conv_in['dw_w'], 'L1_conv_w1': _L1_conv_in['w1'], 'L1_conv_b1': _L1_conv_in['b1'], 'L1_conv_gamma': _L1_conv_in['gamma'], 'L1_conv_beta': _L1_conv_in['beta'], 'L1_conv_w2': _L1_conv_in['w2'], 'L1_conv_b2': _L1_conv_in['b2'], 'L2_conv_w_om': _L2_conv_in['w_om'], 'L2_conv_b_om': _L2_conv_in['b_om'], 'L2_conv_w_dc': _L2_conv_in['w_dc'], 'L2_conv_b_dc': _L2_conv_in['b_dc'], 'L3_conv_Wq': _L3_conv_in['Wq'], 'L3_conv_Wk': _L3_conv_in['Wk'], 'L3_conv_Wv': _L3_conv_in['Wv'], 'L3_conv_Wo': _L3_conv_in['Wo']}

def reference(x, L0_conv_pw_w, L0_conv_off_w, L0_conv_off_b, L0_conv_dw_w, L1_conv_w1, L1_conv_b1, L1_conv_gamma, L1_conv_beta, L1_conv_w2, L1_conv_b2, L2_conv_w_om, L2_conv_b_om, L2_conv_w_dc, L2_conv_b_dc, L3_conv_Wq, L3_conv_Wk, L3_conv_Wv, L3_conv_Wo):
    import jax
    import jax.numpy as jnp

    def _L0_conv_ref(x, pw_w, off_w, off_b, dw_w):
        import jax, jax.numpy as jnp
        import numpy as np
        K = 3
        PAD = 1
        STRIDE = 1
        DIL = 1

        def _bilinear_gather(feat, y, x):
            B, C, H, W = feat.shape
            feat_flat = feat.reshape(B, C, H * W)
            y0 = jnp.floor(y)
            x0 = jnp.floor(x)
            out = jnp.zeros((B, C) + y.shape[1:], feat.dtype)
            for yi in (y0, y0 + 1.0):
                for xi in (x0, x0 + 1.0):
                    wgt = (1.0 - jnp.abs(y - yi)) * (1.0 - jnp.abs(x - xi))
                    valid = (yi >= 0) & (yi <= H - 1) & (xi >= 0) & (xi <= W - 1)
                    yc = jnp.clip(yi, 0, H - 1).astype(jnp.int32)
                    xc = jnp.clip(xi, 0, W - 1).astype(jnp.int32)
                    idx = (yc * W + xc).reshape(B, 1, -1)
                    g = jnp.take_along_axis(feat_flat, idx, axis=2).reshape(B, C, *y.shape[1:])
                    out = out + g * (wgt * valid)[:, None]
            return out
        B, _, H, W = x.shape
        C = pw_w.shape[0]
        xp = jnp.einsum('bchw,oc->bohw', x, pw_w)
        off = jnp.einsum('bchw,oc->bohw', xp, off_w) + off_b[None, :, None, None]
        off = off.reshape(B, K * K, 2, H, W)
        oy, ox = (off[:, :, 0], off[:, :, 1])
        ky, kx = jnp.meshgrid(jnp.arange(K), jnp.arange(K), indexing='ij')
        ky = ky.reshape(-1).astype(jnp.float32)
        kx = kx.reshape(-1).astype(jnp.float32)
        gh = jnp.arange(H, dtype=jnp.float32) * STRIDE - PAD
        gw = jnp.arange(W, dtype=jnp.float32) * STRIDE - PAD
        base_y = gh[None, :, None] + (ky * DIL)[:, None, None]
        base_x = gw[None, None, :] + (kx * DIL)[:, None, None].transpose(0, 2, 1)
        y = base_y[None] + oy
        xc = base_x[None] + ox
        sampled = _bilinear_gather(xp, y, xc)
        out = jnp.einsum('bckhw,ck->bchw', sampled, dw_w.reshape(C, K * K))
        return out

    def _L1_conv_ref(x, w1, b1, gamma, beta, w2, b2):
        import jax, jax.numpy as jnp
        import numpy as np
        C = 128
        K = 7
        PAD = (K - 1) // 2
        RED = 4
        EPS = 1e-05
        B, Cc, H, W = x.shape
        h = jnp.einsum('oc,bchw->bohw', w1, x) + b1[None, :, None, None]
        mu = h.mean(axis=(0, 2, 3))
        var = h.var(axis=(0, 2, 3))
        h = (h - mu[None, :, None, None]) * jax.lax.rsqrt(var + EPS)[None, :, None, None]
        h = h * gamma[None, :, None, None] + beta[None, :, None, None]
        h = jax.nn.relu(h)
        wgt = jnp.einsum('oc,bchw->bohw', w2, h) + b2[None, :, None, None]
        wgt = wgt.reshape(B, Cc, K, K, H, W)
        xp = jnp.pad(x, ((0, 0), (0, 0), (PAD, PAD), (PAD, PAD)))
        out = jnp.zeros_like(x)
        for i in range(K):
            for j in range(K):
                out = out + wgt[:, :, i, j] * xp[:, :, i:i + H, j:j + W]
        return out

    def _L2_conv_ref(x, w_om, b_om, w_dc, b_dc):
        import jax, jax.numpy as jnp
        import numpy as np
        KH, KW = (3, 3)
        K = KH * KW
        PAD, STRIDE, DIL = (1, 1, 1)

        def _conv(x, w, b):
            y = jax.lax.conv_general_dilated(x, w, (STRIDE, STRIDE), ((PAD, PAD), (PAD, PAD)), rhs_dilation=(DIL, DIL), dimension_numbers=('NCHW', 'OIHW', 'NCHW'))
            return y + b[None, :, None, None]

        def _bilinear_gather(x, py, px):
            B, C, H, W = x.shape
            y0 = jnp.floor(py)
            x0 = jnp.floor(px)
            wy1 = py - y0
            wx1 = px - x0
            wy0 = 1.0 - wy1
            wx0 = 1.0 - wx1
            xf = x.reshape(B, C, H * W)

            def g(yi, xi):
                valid = (yi >= 0) & (yi < H) & (xi >= 0) & (xi < W)
                yc = jnp.clip(yi, 0, H - 1).astype(jnp.int32)
                xc = jnp.clip(xi, 0, W - 1).astype(jnp.int32)
                idx = (yc * W + xc).reshape(B, -1)
                v = jax.vmap(lambda im, ix: im[:, ix])(xf, idx)
                v = v.reshape(B, C, *yi.shape[1:])
                return v * valid[:, None].astype(x.dtype)
            return (wy0 * wx0)[:, None] * g(y0, x0) + (wy0 * wx1)[:, None] * g(y0, x0 + 1) + (wy1 * wx0)[:, None] * g(y0 + 1, x0) + (wy1 * wx1)[:, None] * g(y0 + 1, x0 + 1)
        B, C, H, W = x.shape
        om = _conv(x, w_om, b_om)
        offset = om[:, :2 * K].reshape(B, K, 2, H, W)
        mask = jax.nn.sigmoid(om[:, 2 * K:])
        dy, dx = (offset[:, :, 0], offset[:, :, 1])
        kh = jnp.repeat(jnp.arange(KH), KW)
        kw = jnp.tile(jnp.arange(KW), KH)
        ho = jnp.arange(H)
        wo = jnp.arange(W)
        py = ho[None, None, :, None] * STRIDE - PAD + kh[None, :, None, None] * DIL + dy
        px = wo[None, None, None, :] * STRIDE - PAD + kw[None, :, None, None] * DIL + dx
        sampled = _bilinear_gather(x, py, px)
        sampled = sampled * mask[:, None]
        w = w_dc.reshape(w_dc.shape[0], C, K)
        out = jnp.einsum('bckhw,ock->bohw', sampled, w) + b_dc[None, :, None, None]
        return out

    def _L3_conv_ref(x, Wq, Wk, Wv, Wo):
        import jax, jax.numpy as jnp
        import numpy as np
        CHANNEL = 128
        NUM_HEADS = 8
        HEAD_DIM = CHANNEL // NUM_HEADS
        b, c, h, w = x.shape
        s = h * w
        xt = x.reshape(b, c, s).transpose(0, 2, 1)

        def proj(W):
            y = jnp.einsum('bsc,dc->bsd', xt, W)
            return y.reshape(b, s, NUM_HEADS, HEAD_DIM).transpose(0, 2, 1, 3)
        q, k, v = (proj(Wq), proj(Wk), proj(Wv))
        scale = 1.0 / np.sqrt(HEAD_DIM).astype(np.float32)
        scores = jnp.einsum('bhqd,bhkd->bhqk', q, k) * scale
        attn = jax.nn.softmax(scores, axis=-1)
        out = jnp.einsum('bhqk,bhkd->bhqd', attn, v)
        out = out.transpose(0, 2, 1, 3).reshape(b, s, c)
        z = jnp.einsum('bsc,dc->bsd', out, Wo)
        return z.transpose(0, 2, 1).reshape(b, c, h, w)

    def _gn(v, G=32, eps=1e-05):
        B_, C_, H_, W_ = v.shape
        g = v.reshape(B_, G, C_ // G, H_, W_)
        m = jnp.mean(g, axis=(2, 3, 4), keepdims=True)
        s = jnp.var(g, axis=(2, 3, 4), keepdims=True)
        return ((g - m) / jnp.sqrt(s + eps)).reshape(v.shape)

    def _ln_c(v, eps=1e-06):
        m = jnp.mean(v, axis=1, keepdims=True)
        s = jnp.var(v, axis=1, keepdims=True)
        return (v - m) / jnp.sqrt(s + eps)

    def _ln_t(v, eps=1e-05):
        m = jnp.mean(v, axis=-1, keepdims=True)
        s = jnp.var(v, axis=-1, keepdims=True)
        return (v - m) / jnp.sqrt(s + eps)

    def _to_tokens(v):
        B_, C_, H_, W_ = v.shape
        return v.reshape(B_, C_, H_ * W_).transpose(0, 2, 1)

    def _from_tokens(t, like):
        B_, C_, H_, W_ = like.shape
        return t.transpose(0, 2, 1).reshape(B_, C_, H_, W_)
    x = x + _L0_conv_ref(_gn(x), L0_conv_pw_w, L0_conv_off_w, L0_conv_off_b, L0_conv_dw_w)
    x = x + _L1_conv_ref(_gn(x), L1_conv_w1, L1_conv_b1, L1_conv_gamma, L1_conv_beta, L1_conv_w2, L1_conv_b2)
    x = x + _L2_conv_ref(_gn(x), L2_conv_w_om, L2_conv_b_om, L2_conv_w_dc, L2_conv_b_dc)
    x = x + _L3_conv_ref(_gn(x), L3_conv_Wq, L3_conv_Wk, L3_conv_Wv, L3_conv_Wo)
    return x

_drawn_inputs = setup_inputs


def setup_inputs(seed=0):
    import zlib

    import numpy as np

    out = dict(_drawn_inputs(seed))
    spreads = {'L1_conv_b1': (0.0, 0.8),
     'L1_conv_gamma': (1.0, 0.2),
     'L1_conv_beta': (0.0, 0.1),
     'L1_conv_b2': (0.0, 0.1),
     'L2_conv_b_om': (0.0, 0.1),
     'L2_conv_b_dc': (0.0, 0.1)}
    factors = {'L3_conv_Wq': 8.0, 'L3_conv_Wk': 8.0, 'L3_conv_Wv': 6.014, 'L3_conv_Wo': 5.699}
    for name, (base, spread) in spreads.items():
        noise = np.random.default_rng([zlib.crc32(name.encode()), seed]).standard_normal(out[name].shape)
        drawn = base * np.exp(spread * noise) if base else spread * noise
        out[name] = jnp.asarray(drawn.astype(out[name].dtype))
    for name, factor in factors.items():
        out[name] = (out[name] * factor).astype(out[name].dtype)
    return out
```

```python
from contextlib import ExitStack

import numpy as np

import concourse.bass as bass
from concourse import mybir

F32 = mybir.dt.float32
BF16 = mybir.dt.bfloat16
I32 = mybir.dt.int32
ALU = mybir.AluOpType
ACT = mybir.ActivationFunctionType
AX = mybir.AxisListType

B, C, H, W = 2, 128, 48, 48
S = H * W
N = B * S
GROUP = 4
ROWS = 8
CH = ROWS * W
NCH = S // CH
BANK = 512

K2 = 9
PW = 50
QT = 20
QN = QT * 128
GUARD = 64
TROWS = QN + GUARD
CORNERS = (0, 1, PW, PW + 1)
TILES = S // 128
SLOTS = 2

K7 = 7
TAPS = K7 * K7
RED = 32
IW = W + K7 - 1
IN = IW * IW
TG = 3
NTG = (TAPS + TG - 1) // TG

HEADS, HD = 8, 16
NH = B * HEADS
KT = S // 128
QC = CH
NQC = S // QC
CHUNKS = NH * NQC
PAIR = 2 * NQC
Q_PARTS = (0, 0, 0, 1, 1, 2)
K_PARTS = (0, 1, 2, 0, 1, 0)
KROWS = len(Q_PARTS) * HD
MROWS = 3
ERING = 4


class Chain:

    def __init__(self, eng, sem):
        self.eng, self.sem, self.count, self.base = eng, sem, 0, 0

    def link(self, ins):
        self.count += 1
        ins.then_inc(self.sem, 1)
        self.eng.wait_ge(self.sem, self.base + self.count)


def semaphores(ctx, nc, prefix, names):
    return {n: ctx.enter_context(nc.semaphore(f"{prefix}_{n}")) for n in names.split()}


GN_SEMS = "stats means var std norm gchain gst "


def norm_vector(nc, dve, s, t, write):
    chain = Chain(dve, s["gchain"])
    for b in range(B):
        for q in range(NCH):
            last = nc.vector.bn_stats(t["bst"][:, b, q, :], t["x"][:, b * S + q * CH:b * S + (q + 1) * CH])
    chain.link(last)
    for b in range(B):
        last = nc.vector.bn_aggr(t["mv"][:, b, :], t["bst"][:, b, :, :].rearrange("p q e -> p (q e)"))
    chain.link(last)
    chain.link(nc.vector.tensor_tensor(t["msq"][:, :], t["mv"][:, :, 0], t["mv"][:, :, 0], ALU.mult))
    nc.vector.tensor_tensor(t["mv"][:, :, 1], t["mv"][:, :, 1], t["msq"][:, :], ALU.add).then_inc(s["stats"], 1)
    dve.wait_ge(s["means"], 1)
    chain.link(nc.vector.tensor_copy(t["gm"][:, :, :].rearrange("p b e -> p (b e)"), t["ps"][:, 0, 0:2 * B]))
    chain.link(nc.vector.tensor_tensor(t["msq"][:, :], t["gm"][:, :, 0], t["gm"][:, :, 0], ALU.mult))
    nc.vector.tensor_tensor(t["var"][:, :], t["gm"][:, :, 1], t["msq"][:, :], ALU.subtract).then_inc(s["var"], 1)
    dve.wait_ge(s["std"], 1)
    chain.link(nc.vector.reciprocal(t["rstd"][:, :], t["std"][:, :]))
    for b in range(B):
        write(b, t["gm"][:, b, 0:1], t["rstd"][:, b:b + 1]).then_inc(s["norm"], 1)


def norm_tensor(nc, pe, s, t):
    pe.wait_ge(s["stats"], 1)
    nc.tensor.matmul(t["ps"][:, 0, 0:2 * B], t["gavg"][:, :], t["mv"][:, :, :].rearrange("p b e -> p (b e)"),
                     start=True, stop=True).then_inc(s["means"], 1)


def norm_scalar(nc, act, s, t):
    act.wait_ge(s["var"], 1)
    nc.scalar.activation(t["std"][:, :], t["var"][:, :], ACT.Sqrt, bias=t["eps"][:, 0:1]).then_inc(s["std"], 1)


def window(img, b, r, ky, kx):
    at = (ROWS * r + ky) * PW + kx
    return img[:, b, at:at + ROWS * PW].rearrange("p (r w) -> p r w", w=PW)[:, :, 0:W]


SAMPLE_SEMS = GN_SEMS + ("zeroed pw_mm image off_mm offs tok_mm tok ot_mm mask chain index table0 table1 "
                         "gap gaps copied gather0 gather1 first_corner summed turned_mm turned out_mm added diag passed")


def sampling_layer(nc, g, modulated):
    R = 27 if modulated else 18
    with ExitStack() as ctx:
        def sb(name, shape, dt=F32):
            return ctx.enter_context(nc.sbuf_tensor(f"l{2 * modulated}_{name}", shape, dt))

        s = semaphores(ctx, nc, f"l{2 * modulated}", SAMPLE_SEMS)
        t = g
        ps = g["ps"]
        img = sb("img", [128, B, QN])
        offc = sb("offc", [R, N])
        tok = sb("tok", [128, B, QT, 128])
        yx = sb("yx", [128, TILES * K2, 2])
        fl = sb("fl", [128, TILES * K2, 2])
        ri = sb("ri", [128, TILES * K2, 2], I32)
        gt = sb("gt", [128, TILES * K2, 2])
        fr = sb("fr", [128, TILES * K2, 2])
        mk = sb("mk", [128, B, TILES * K2])
        qi = sb("qi", [128, TILES * K2])
        idx = sb("idx", [128, B * TILES * K2], I32)
        wts = sb("wts", [128, B * TILES * K2 * 4])
        idx_s = sb("idx_s", [128, SLOTS, K2], I32)
        wts_s = sb("wts_s", [128, SLOTS, K2 * 4])
        corner = sb("corner", [128, SLOTS, K2, 4 * 128])
        samp = sb("samp", [128, SLOTS, K2, 128])
        turned = sb("turned", [128, SLOTS, K2 * 128])
        if modulated:
            wk, offw, offb = g["w_dc"], g["w_om"], g["b_om"]
        else:
            wk = sb("wk", [128, K2, 128])
            offw, offb = g["off_w"], g["off_b"]
            xg = sb("xg", [128, N])
        gap = sb("gap", [GUARD, 4 * 128])
        table = [nc.dram_tensor(f"table{2 * modulated}_{b}", [TROWS, 4 * 128], F32).ap() for b in range(B)]
        gather = [s["gather0"], s["gather1"]]
        filled = [s["table0"], s["table1"]]

        with nc.Block() as block:

            @block.gpsimd
            def _(pool):
                nc.gpsimd.memset(gap[:, :], 0.0).then_inc(s["gap"], 1)
                nc.gpsimd.memset(img[:, :, :], 0.0).then_inc(s["zeroed"], 1)

                def tile(b, i, slot):
                    pool.wait_ge(s["summed"], 3 * i + 3)
                    nc.gpsimd.tensor_copy(idx_s[:, slot, :], idx[:, bass.ds(i * K2, K2)])
                    nc.gpsimd.tensor_copy(wts_s[:, slot, :], wts[:, bass.ds(i * K2 * 4, K2 * 4)]) \
                        .then_inc(s["copied"], 1)
                    pool.wait_ge(s["copied"], i + 1)
                    pool.sem_inc(s["passed"], 1)
                    for k in range(K2):
                        nc.gpsimd.indirect_dma_start(
                            corner[:, slot, k, :], None, table[b],
                            bass.IndirectOffsetOnAxis(ap=idx_s[:, slot, k:k + 1], axis=0),
                        ).then_inc(gather[slot], 16)

                for b in range(B):
                    pool.wait_ge(filled[b], 16 * len(CORNERS))
                    pool.wait_ge(s["index"], b + 1)
                    with pool.Fori(b * TILES // 2, (b + 1) * TILES // 2) as turn:
                        for slot in range(SLOTS):
                            tile(b, turn * SLOTS + slot, slot)

            @block.sync
            def _(sp):
                sp.wait_ge(s["gap"], 1)
                for b in range(B):
                    sp.dma_start(table[b][0:GUARD, :], gap[:, :]).then_inc(s["gaps"], 16)
                    sp.dma_start(table[b][QN:TROWS, :], gap[:, :]).then_inc(s["gaps"], 16)
                sp.wait_ge(s["gaps"], 16 * 2 * B)
                for b in range(B):
                    sp.wait_ge(s["tok"], (b + 1) * QT // 4)
                    for j, d in enumerate(CORNERS):
                        lo = GUARD - d
                        sp.dma_start(table[b][lo:lo + QN, j * 128:(j + 1) * 128]
                                     .rearrange("(t p) c -> p t c", p=128),
                                     tok[:, b, :, :]).then_inc(filled[b], 16)
                for b in range(B):
                    sp.wait_ge(filled[b], 16 * len(CORNERS))

            @block.scalar
            def _(act):
                norm_scalar(nc, act, s, t)
                act.wait_ge(s["zeroed"], 1)
                for b in range(B):
                    if not modulated:
                        for r in range(NCH):
                            n = b * NCH + r
                            act.wait_ge(s["pw_mm"], n + 1)
                            nc.scalar.copy(window(img, b, r, 1, 1),
                                           ps[:, n % 2, 0:CH].rearrange("p (r w) -> p r w", w=W)) \
                                .then_inc(s["image"], 1)
                    for r in range(NCH):
                        n = b * NCH + r
                        act.wait_ge(s["off_mm"], n + 1)
                        nc.scalar.activation(offc[:, n * CH:(n + 1) * CH], ps[0:R, 2 + n % 2, 0:CH],
                                             ACT.Identity, bias=offb[:, 0:1]).then_inc(s["offs"], 1)
                    for q in range(QT // 4):
                        n = b * (QT // 4) + q
                        act.wait_ge(s["tok_mm"], n + 1)
                        nc.scalar.copy(tok[:, b, 4 * q:4 * q + 4, :].rearrange("p t c -> p (t c)"),
                                       ps[:, 4 + n % 2, :]).then_inc(s["tok"], 1)
                    if modulated:
                        act.wait_ge(s["ot_mm"], b + 1)
                        nc.scalar.activation(
                            mk[:, b, :].rearrange("p (t k) -> p t k", k=K2),
                            ps[:, 6 + b, 0:TILES * R].rearrange("p (t r) -> p t r", r=R)[:, :, 2 * K2:R],
                            ACT.Sigmoid).then_inc(s["mask"], 1)

                act.sem_inc(s["turned"], SLOTS)
                with act.Fori(0, B * TILES // 2) as turn:
                    for slot in range(SLOTS):
                        i = turn * SLOTS + slot
                        act.wait_ge(gather[slot], turn * (16 * K2) + 16 * K2)
                        act.wait_ge(s["turned_mm"], i + 1)
                        for k in range(K2):
                            last = nc.scalar.activation(samp[:, slot, k, :], corner[:, slot, k, 0:128],
                                                        ACT.Copy, scale=wts_s[:, slot, 4 * k:4 * k + 1])
                        last.then_inc(s["first_corner"], 1)
                    for slot in range(SLOTS):
                        i = turn * SLOTS + slot
                        act.wait_ge(s["turned_mm"], i + 1 + SLOTS)
                        act.wait_ge(s["out_mm"], i + 1)
                        nc.scalar.copy(turned[:, slot, :].rearrange("p (a n) -> p a n", a=3),
                                       ps[:, 3 * slot:3 * slot + 3, 0:CH]).then_inc(s["turned"], 1)

            @block.vector
            def _(dve):
                if modulated:
                    dve.wait_ge(s["zeroed"], 1)

                    def write(b, mean, rstd):
                        return nc.vector.tensor_scalar(
                            img[:, b, PW + 1:PW + 1 + H * PW].rearrange("p (r w) -> p r w", w=PW)[:, :, 0:W],
                            g["x"][:, b * S:(b + 1) * S].rearrange("p (r w) -> p r w", w=W),
                            mean, rstd, ALU.subtract, ALU.mult)
                else:
                    def write(b, mean, rstd):
                        return nc.vector.tensor_scalar(xg[:, b * S:(b + 1) * S], g["x"][:, b * S:(b + 1) * S],
                                                       mean, rstd, ALU.subtract, ALU.mult)
                norm_vector(nc, dve, s, t, write)
                if not modulated:
                    for k in range(K2):
                        last = nc.vector.tensor_scalar(wk[:, k, :], g["ident"][:, :], g["dw"][:, k:k + 1], None,
                                                       ALU.mult)
                    last.then_inc(s["diag"], 1)
                chain = Chain(dve, s["chain"])
                for b in range(B):
                    dve.wait_ge(s["ot_mm"], b + 1)
                    if modulated:
                        dve.wait_ge(s["mask"], b + 1)
                    chain.link(nc.vector.tensor_tensor(
                        yx[:, :, :].rearrange("p (t k) e -> p t (k e)", k=K2),
                        ps[:, 6 + b, 0:TILES * R].rearrange("p (t r) -> p t r", r=R)[:, :, 0:2 * K2],
                        g["base"][:, :].rearrange("p (t r) -> p t r", r=2 * K2), ALU.add))
                    chain.link(nc.vector.tensor_scalar(yx[:, :, :], yx[:, :, :], -1.0, float(H),
                                                       ALU.max, ALU.min))
                    chain.link(nc.vector.tensor_copy(ri[:, :, :], yx[:, :, :]))
                    chain.link(nc.vector.tensor_copy(fl[:, :, :], ri[:, :, :]))
                    chain.link(nc.vector.tensor_tensor(gt[:, :, :], fl[:, :, :], yx[:, :, :], ALU.is_gt))
                    chain.link(nc.vector.tensor_tensor(fl[:, :, :], fl[:, :, :], gt[:, :, :], ALU.subtract))
                    chain.link(nc.vector.tensor_tensor(fr[:, :, :], yx[:, :, :], fl[:, :, :], ALU.subtract))
                    chain.link(nc.vector.tensor_scalar(gt[:, :, :], fr[:, :, :], -1.0, 1.0, ALU.mult, ALU.add))
                    if modulated:
                        chain.link(nc.vector.tensor_tensor(gt[:, :, 0], gt[:, :, 0], mk[:, b, :], ALU.mult))
                        chain.link(nc.vector.tensor_tensor(fr[:, :, 0], fr[:, :, 0], mk[:, b, :], ALU.mult))
                    w4 = wts[:, b * TILES * K2 * 4:(b + 1) * TILES * K2 * 4] \
                        .rearrange("p (n j) -> p n j", j=4)
                    for j, (wy, wx) in enumerate(((gt, gt), (gt, fr), (fr, gt), (fr, fr))):
                        nc.vector.tensor_tensor(w4[:, :, j], wy[:, :, 0], wx[:, :, 1], ALU.mult)
                    chain.link(nc.vector.scalar_tensor_tensor(qi[:, :], fl[:, :, 0], float(PW), fl[:, :, 1],
                                                              ALU.mult, ALU.add))
                    last = nc.vector.tensor_scalar(idx[:, b * TILES * K2:(b + 1) * TILES * K2], qi[:, :],
                                                   float(GUARD + PW + 1), None, ALU.add)
                    last.then_inc(s["index"], 1)
                    dve.wait_ge(s["index"], b + 1)

                dve.sem_inc(s["summed"], 3 * SLOTS)
                dve.sem_inc(s["added"], SLOTS)
                with dve.Fori(0, B * TILES // 2) as turn:
                    for slot in range(SLOTS):
                        i = turn * SLOTS + slot
                        dve.wait_ge(s["first_corner"], i + 1)
                        for j in range(1, 4):
                            for k in range(K2):
                                last = nc.vector.scalar_tensor_tensor(
                                    samp[:, slot, k, :], corner[:, slot, k, j * 128:(j + 1) * 128],
                                    wts_s[:, slot, 4 * k + j:4 * k + j + 1], samp[:, slot, k, :],
                                    ALU.mult, ALU.add)
                            last.then_inc(s["summed"], 1)
                            if j < 3:
                                dve.wait_ge(s["summed"], 3 * i + 3 * SLOTS + j)
                    for slot in range(SLOTS):
                        i = turn * SLOTS + slot
                        dve.wait_ge(s["out_mm"], i + 1 + SLOTS)
                        xt = g["x"][:, bass.ds(i * 128, 128)]
                        if modulated:
                            ins = nc.vector.scalar_tensor_tensor(xt, ps[:, 6 + slot, 0:128], g["b_dc"][:, 0:1], xt,
                                                                 ALU.add, ALU.add)
                        else:
                            ins = nc.vector.tensor_tensor(xt, ps[:, 6 + slot, 0:128], xt, ALU.add)
                        ins.then_inc(s["added"], 1)

            @block.tensor
            def _(pe):
                norm_tensor(nc, pe, s, t)
                for b in range(B):
                    pe.wait_ge(s["norm"], b + 1)
                    if not modulated:
                        for r in range(NCH):
                            n = b * NCH + r
                            if n >= 2:
                                pe.wait_ge(s["image"], n - 1)
                            nc.tensor.matmul(ps[:, n % 2, 0:CH], g["pw"][:, :], xg[:, n * CH:(n + 1) * CH],
                                             start=True, stop=True).then_inc(s["pw_mm"], 1)
                        pe.wait_ge(s["image"], (b + 1) * NCH)
                    for r in range(NCH):
                        n = b * NCH + r
                        if n >= 2:
                            pe.wait_ge(s["offs"], n - 1)
                        if modulated:
                            for k in range(K2):
                                last = nc.tensor.matmul(ps[0:R, 2 + n % 2, 0:CH], offw[:, k, :],
                                                        window(img, b, r, k // 3, k % 3),
                                                        start=(k == 0), stop=(k == K2 - 1))
                        else:
                            last = nc.tensor.matmul(ps[0:R, 2 + n % 2, 0:CH], offw[:, :],
                                                    window(img, b, r, 1, 1), start=True, stop=True)
                        last.then_inc(s["off_mm"], 1)
                    for q in range(QT // 4):
                        n = b * (QT // 4) + q
                        if n >= 2:
                            pe.wait_ge(s["tok"], n - 1)
                        for j in range(4):
                            at = (4 * q + j) * 128
                            last = nc.tensor.transpose(ps[:, 4 + n % 2, j * 128:(j + 1) * 128],
                                                       img[:, b, at:at + 128], g["ident"][:, :])
                        last.then_inc(s["tok_mm"], 1)
                    pe.wait_ge(s["offs"], (b + 1) * NCH)
                    for i in range(TILES):
                        at = b * S + i * 128
                        last = nc.tensor.transpose(ps[:, 6 + b, i * R:(i + 1) * R], offc[:, at:at + 128],
                                                   g["ident"][0:R, 0:R])
                    last.then_inc(s["ot_mm"], 1)

                pe.wait_ge(s["tok"], B * QT // 4)
                pe.wait_ge(s["index"], B)
                if not modulated:
                    pe.wait_ge(s["diag"], 1)
                pe.sem_inc(s["turned_mm"], SLOTS)
                pe.sem_inc(s["out_mm"], SLOTS)
                with pe.Fori(0, B * TILES // 2) as turn:
                    for slot in range(SLOTS):
                        i = turn * SLOTS + slot
                        pe.wait_ge(s["summed"], 3 * i + 3 * SLOTS + 3)
                        pe.wait_ge(s["turned"], i + 1)
                        for k in range(K2):
                            last = nc.tensor.transpose(ps[:, 3 * slot + k // 3, (k % 3) * 128:(k % 3 + 1) * 128],
                                                       samp[:, slot, k, :], g["ident"][:, :])
                        last.then_inc(s["turned_mm"], 1)
                        pe.wait_ge(s["turned"], i + 1 + SLOTS)
                        pe.wait_ge(s["added"], i + 1)
                        for k in range(K2):
                            last = nc.tensor.matmul(ps[:, 6 + slot, 0:128], wk[:, k, :],
                                                    turned[:, slot, k * 128:(k + 1) * 128],
                                                    start=(k == 0), stop=(k == K2 - 1))
                        last.then_inc(s["out_mm"], 1)


INV_SEMS = GN_SEMS + ("zeroed padded red_mm red rstats rvar rstd rnorm chain relu wgt_mm products acc_used "
                      "acc_mm added pairs")


def involution_layer(nc, g):
    with ExitStack() as ctx:
        def sb(name, shape, dt=F32):
            return ctx.enter_context(nc.sbuf_tensor(f"l1_{name}", shape, dt))

        s = semaphores(ctx, nc, "l1", INV_SEMS)
        ps = g["ps"]
        RP = TG * RED
        xg = sb("xg", [128, N])
        pad = sb("pad", [128, B, IN])
        red = sb("red", [RP, N])
        rst = sb("rst", [RP, B * NCH * 6])
        rmv = sb("rmv", [RP, 2])
        rsd = sb("rsd", [RP, 1])
        rrs = sb("rrs", [RP, 1])
        scale = sb("scale", [RP, 1])
        shift = sb("shift", [RP, 1])
        act_c = sb("act_c", [RP, CH])
        prod = sb("prod", [128, 2, TG, CH])
        ACC = 6

        with nc.Block() as block:

            @block.gpsimd
            def _(pool):
                nc.gpsimd.memset(pad[:, :, :], 0.0).then_inc(s["zeroed"], 1)

            @block.scalar
            def _(act):
                norm_scalar(nc, act, s, g)
                act.wait_ge(s["zeroed"], 1)
                for b in range(B):
                    act.wait_ge(s["norm"], b + 1)
                    nc.scalar.copy(pad[:, b, 3 * IW:3 * IW + H * IW].rearrange("p (r w) -> p r w", w=IW)[:, :, 3:3 + W],
                                   xg[:, b * S:(b + 1) * S].rearrange("p (r w) -> p r w", w=W)) \
                        .then_inc(s["padded"], 1)
                for n in range(B * NCH):
                    act.wait_ge(s["red_mm"], n + 1)
                    nc.scalar.activation(red[:, n * CH:(n + 1) * CH], ps[0:RP, n % 2, 0:CH], ACT.Identity,
                                         bias=g["b1"][:, 0:1]).then_inc(s["red"], 1)
                act.wait_ge(s["rvar"], 1)
                nc.scalar.activation(rsd[:, :], rmv[:, 1:2], ACT.Sqrt, bias=g["eps"][0:RP, 0:1]).then_inc(s["rstd"], 1)
                act.wait_ge(s["rnorm"], 1)
                with act.Fori(0, B * NCH) as c:
                    act.wait_ge(s["wgt_mm"], NTG * c + 1)
                    nc.scalar.activation(act_c[:, :], red[:, bass.ds(c * CH, CH)], ACT.Relu,
                                         bias=shift[:, 0:1], scale=scale[:, 0:1]).then_inc(s["relu"], 1)

            @block.vector
            def _(dve):
                def write(b, mean, rstd):
                    return nc.vector.tensor_scalar(xg[:, b * S:(b + 1) * S], g["x"][:, b * S:(b + 1) * S],
                                                   mean, rstd, ALU.subtract, ALU.mult)
                norm_vector(nc, dve, s, g, write)
                chain = Chain(dve, s["chain"])
                for n in range(B * NCH):
                    dve.wait_ge(s["red"], n + 1)
                    last = nc.vector.bn_stats(rst[:, n * 6:(n + 1) * 6], red[:, n * CH:(n + 1) * CH])
                chain.link(last)
                nc.vector.bn_aggr(rmv[:, :], rst[:, :]).then_inc(s["rvar"], 1)
                dve.wait_ge(s["rstd"], 1)
                chain.link(nc.vector.reciprocal(rrs[:, :], rsd[:, :]))
                chain.link(nc.vector.tensor_tensor(scale[:, :], rrs[:, :], g["gamma"][:, :], ALU.mult))
                chain.link(nc.vector.tensor_tensor(shift[:, :], rmv[:, 0:1], scale[:, :], ALU.mult))
                nc.vector.tensor_tensor(shift[:, :], g["beta"][:, :], shift[:, :], ALU.subtract).then_inc(s["rnorm"], 1)
                dve.wait_ge(s["padded"], B)
                dve.sem_inc(s["products"], 2)
                dve.sem_inc(s["added"], 1)
                with dve.Fori(0, B) as b:
                    with dve.Fori(0, NCH) as r:
                        c = b * NCH + r
                        for q in range(NTG):
                            taps = range(TG * q, min(TG * q + TG, TAPS))
                            dve.wait_ge(s["wgt_mm"], NTG * c + q + 2)
                            dve.wait_ge(s["acc_used"], NTG * c + q + (2 if q == 0 else 1))
                            for j, k in enumerate(taps):
                                src = pad[:, :, :].rearrange("p b n -> p (b n)")[
                                    :, bass.ds(b * IN + r * (ROWS * IW) + (k // K7) * IW, ROWS * IW)] \
                                    .rearrange("p (r w) -> p r w", w=IW)[:, :, k % K7:k % K7 + W]
                                last = nc.vector.scalar_tensor_tensor(
                                    prod[:, q % 2, j, :].rearrange("p (r w) -> p r w", w=W),
                                    ps[:, TG * (q % 2) + j, 0:CH].rearrange("p (r w) -> p r w", w=W),
                                    g["b2"][:, k:k + 1], src, ALU.add, ALU.mult)
                            if len(taps) == TG:
                                last.then_inc(s["pairs"], 1)
                                dve.wait_ge(s["pairs"], (NTG - 1) * c + q + 1)
                                last = nc.vector.tensor_tensor(prod[:, q % 2, 0, :], prod[:, q % 2, 0, :],
                                                               prod[:, q % 2, 1, :], ALU.add)
                            last.then_inc(s["products"], 1)
                        dve.wait_ge(s["acc_mm"], c + 1)
                        xt = g["x"][:, bass.ds(c * CH, CH)]
                        nc.vector.tensor_tensor(xt, ps[:, ACC, 0:CH], xt, ALU.add).then_inc(s["added"], 1)

            @block.tensor
            def _(pe):
                norm_tensor(nc, pe, s, g)
                for n in range(B * NCH):
                    pe.wait_ge(s["norm"], n // NCH + 1)
                    if n >= 2:
                        pe.wait_ge(s["red"], n - 1)
                    nc.tensor.matmul(ps[0:RP, n % 2, 0:CH], g["w1"][:, :], xg[:, n * CH:(n + 1) * CH],
                                     start=True, stop=True).then_inc(s["red_mm"], 1)
                pe.wait_ge(s["red"], B * NCH)
                pe.sem_inc(s["wgt_mm"], 1)
                pe.sem_inc(s["acc_used"], 2)
                with pe.Fori(0, B * NCH) as c:
                    pe.wait_ge(s["relu"], c + 1)

                    def weights(q):
                        pe.wait_ge(s["products"], NTG * c + q + (2 if q == 0 else 1))
                        for j, k in enumerate(range(TG * q, min(TG * q + TG, TAPS))):
                            last = nc.tensor.matmul(ps[:, TG * (q % 2) + j, 0:CH], g["w2"][RED * j:RED * (j + 1), q, :],
                                                    act_c[RED * j:RED * (j + 1), :], start=True, stop=True)
                        last.then_inc(s["wgt_mm"], 1)

                    def add(q):
                        pe.wait_ge(s["products"], NTG * c + q + 3)
                        if q == 0:
                            pe.wait_ge(s["added"], c + 1)
                        js = (0, 2) if TG * q + TG <= TAPS else (0,)
                        for j in js:
                            last = nc.tensor.matmul(ps[:, ACC, 0:CH], g["ident"][:, :], prod[:, q % 2, j, :],
                                                    start=(q == 0 and j == 0), stop=(q == NTG - 1))
                        last.then_inc(s["acc_used"], 1)

                    for q in range(NTG):
                        weights(q)
                        if q:
                            add(q - 1)
                    add(NTG - 1)
                    pe.wait_ge(s["acc_used"], NTG * c + NTG + 2)
                    pe.sem_inc(s["acc_mm"], 1)


ATT_SEMS = GN_SEMS + ("const proj part1 part2 split v_mm v_all stored loaded0 loaded1 v_slot st_mm exp av_mm "
                      "a_mm max negmax nsplit rows_mm rows o_sb ot_mm ochain out z_in zt_mm zt z_mm z_added saved "
                      "pchain passed")


def attention_layer(nc, g, out):
    with ExitStack() as ctx:
        def sb(name, shape, dt=F32):
            return ctx.enter_context(nc.sbuf_tensor(f"l3_{name}", shape, dt))

        s = semaphores(ctx, nc, "l3", ATT_SEMS)
        ps = g["ps"]
        xg = sb("xg", [128, N])
        part = sb("part", [128, 2, 3, S], BF16)
        rest = sb("rest", [128, 2, CH])
        v_all = sb("v_all", [128, NH, KT, HD])
        v_s = sb("v_s", [128, 2, KT, 32])
        qs = sb("qs", [KROWS + MROWS, 2, S], BF16)
        ks = sb("ks", [KROWS + MROWS, 2, S], BF16)
        e = sb("e", [128, ERING, QC])
        mx = sb("mx", [128, 2, 3, NQC])
        nm = sb("nm", [128, 2, 3])
        nr = sb("nr", [128, 2, 3])
        nsp = sb("nsp", [128, 2, 3, MROWS], BF16)
        identb = sb("identb", [128, 128], BF16)
        o_s = sb("o_s", [128, 2, 96])
        rec = sb("rec", [96, 4])
        o_t = sb("o_t", [96, 1 + CHUNKS, 4, HD])
        z_in = sb("z_in", [96, 2, 4, C])
        z_t = sb("z_t", [128, 2, CH])
        stack = nc.dram_tensor("qk_parts", [2 * 3 * B * 128, S], BF16).ap()
        ST, AB, AV, MISC = 0, 3, 5, 7
        loaded = [s["loaded0"], s["loaded1"]]
        LOADS = 16 * 2 * len(Q_PARTS)

        with nc.Block() as block:

            @block.sync
            def _(sp):
                for b in range(B):
                    for side in range(2):
                        sp.wait_ge(s["split"], (2 * b + side + 1) * NCH)
                        for p in range(3):
                            r0 = (side * 3 + p) * B * 128 + b * 128
                            sp.dma_start(stack[r0:r0 + 128, :], part[:, side, p, :]).then_inc(s["stored"], 16)
                sp.wait_ge(s["stored"], 16 * 3 * 2 * B)

                def load(n, slot):
                    for side, (tile, parts) in enumerate(((qs, Q_PARTS), (ks, K_PARTS))):
                        for i, p in enumerate(parts):
                            sp.dma_start(tile[HD * i:HD * (i + 1), slot, :],
                                         stack[bass.ds(n * HD + (side * 3 + p) * B * 128, HD), :]) \
                                .then_inc(loaded[slot], 16)

                load(0, 0)
                load(1, 1)
                with sp.Fori(0, NH // 2 - 1) as m:
                    for slot in range(2):
                        sp.wait_ge(s["st_mm"], m * (2 * NQC * KT) + (slot + 1) * NQC * KT)
                        load(m * 2 + (2 + slot), slot)
                for c in range(B * NCH):
                    sp.wait_ge(s["z_added"], c + 1)
                    b, r = divmod(c, NCH)
                    sp.dma_start(out[b, :, r * CH:(r + 1) * CH], g["x"][:, c * CH:(c + 1) * CH]).then_inc(s["saved"], 16)
                sp.wait_ge(s["saved"], 16 * B * NCH)

            @block.gpsimd
            def _(pool):
                chain = Chain(pool, s["pchain"])
                chain.link(nc.gpsimd.memset(v_s[:, :, :, HD:32], 0.0))
                chain.link(nc.gpsimd.memset(ks[KROWS:KROWS + MROWS, :, :], 1.0))
                chain.link(nc.gpsimd.memset(o_s[:, :, :], 1.0))
                chain.link(nc.gpsimd.tensor_copy(identb[:, :], g["ident"][:, :]))
                nc.gpsimd.memset(v_s[:, :, :, HD:HD + 1], 1.0).then_inc(s["const"], 1)
                pool.wait_ge(s["v_all"], N // 128)

                def take_v(n, slot):
                    nc.gpsimd.tensor_copy(
                        v_s[:, slot, :, 0:HD],
                        v_all[:, :, :, :].rearrange("p n t d -> p (n t d)")[:, bass.ds(n * (KT * HD), KT * HD)]
                        .rearrange("p (t d) -> p t d", d=HD)).then_inc(s["v_slot"], 1)

                take_v(0, 0)
                pool.wait_ge(s["const"], 1)
                def split_max(ga, slot):
                    pool.wait_ge(s["negmax"], ga + 1)
                    pool.sem_inc(s["passed"], 1)
                    n1, n2, n3 = (nsp[:, slot, :, i] for i in range(3))
                    chain.link(nc.gpsimd.tensor_copy(n1, nm[:, slot, :]))
                    chain.link(nc.gpsimd.tensor_tensor(nr[:, slot, :], nm[:, slot, :], n1, ALU.subtract))
                    pool.sem_inc(s["passed"], 1)
                    chain.link(nc.gpsimd.tensor_copy(n2, nr[:, slot, :]))
                    nc.gpsimd.tensor_tensor(n3, nr[:, slot, :], n2, ALU.subtract).then_inc(s["nsplit"], 1)

                split_max(0, 0)
                split_max(1, 1)

                def pair(m, last):
                    for j in range(PAIR):
                        gq = m * PAIR + j
                        if j % NQC == 1 and not (last and j > NQC):
                            n = m * 2 + j // NQC
                            pool.wait_ge(s["av_mm"], n * (NQC * KT) + ERING)
                            pool.sem_inc(s["passed"], 1)
                            take_v(n + 1, (j // NQC + 1) % 2)
                        if not (last and j >= PAIR - 2):
                            pool.wait_ge(s["rows_mm"], gq + 1)
                            split_max(gq + 2, j % 2)

                start, links = chain.count, 3 * PAIR
                with pool.Fori(0, NH // 2 - 1) as m:
                    chain.base = m * links
                    pair(m, False)
                assert chain.count == start + links
                chain.base, chain.count = 0, start + links * (NH // 2 - 1)
                pair(NH // 2 - 1, True)
                pool.wait_ge(s["out"], CHUNKS + 2)
                for c in range(B * NCH):
                    b, r = divmod(c, NCH)
                    if c >= 2:
                        pool.wait_ge(s["zt_mm"], c - 1)
                    g0 = 1 + b * HEADS * NQC + r
                    nc.gpsimd.tensor_copy(
                        z_in[:, c % 2, :, :].rearrange("p i (h d) -> p i h d", d=HD),
                        o_t[:, g0:g0 + (HEADS - 1) * NQC + 1:NQC, :, :].rearrange("p h i d -> p i h d")) \
                        .then_inc(s["z_in"], 1)

            @block.scalar
            def _(act):
                norm_scalar(nc, act, s, g)
                for b in range(B):
                    for side in range(2):
                        for r in range(NCH):
                            n = (2 * b + side) * NCH + r
                            act.wait_ge(s["proj"], n + 1)
                            if b and r == 0:
                                act.wait_ge(s["stored"], 16 * 3 * 2 * b)
                            nc.scalar.activation(part[:, side, 0, r * CH:(r + 1) * CH], ps[:, n % 2, 0:CH],
                                                 ACT.Copy, scale=HD ** -0.5 if side == 0 else 1.0) \
                                .then_inc(s["part1"], 1)
                for n in range(N // 128):
                    b, t = divmod(n, TILES)
                    act.wait_ge(s["v_mm"], n + 1)
                    nc.scalar.copy(v_all[:, b * HEADS:(b + 1) * HEADS, t, :],
                                   ps[:, 2 + n % 2, 0:128].rearrange("p (h d) -> p h d", d=HD)) \
                        .then_inc(s["v_all"], 1)
                act.wait_ge(s["const"], 1)
                act.sem_inc(s["exp"], ERING)
                act.sem_inc(s["o_sb"], 2)

                def exp(step, bank, slot):
                    act.wait_ge(s["st_mm"], step + 1)
                    act.wait_ge(s["av_mm"], step + 1)
                    nc.scalar.activation(e[:, slot, :], ps[:, ST + bank, 0:QC], ACT.Exp).then_inc(s["exp"], 1)

                def rows(gr, head_slot, c):
                    act.wait_ge(s["rows_mm"], gr + 1)
                    nc.scalar.copy(qs[KROWS:KROWS + MROWS, head_slot, c * QC:(c + 1) * QC],
                                   ps[KROWS:KROWS + MROWS, MISC, 0:QC]).then_inc(s["rows"], 1)

                rows(0, 0, 0)
                for kt in range(2):
                    exp(kt, kt, kt)

                def pair(m, last):
                    for j in range(PAIR):
                        gq = m * PAIR + j
                        end = last and j == PAIR - 1
                        for kt in range(KT):
                            if not (end and kt + 2 >= KT):
                                exp(gq * KT + (kt + 2), (kt + 2) % 3, (j * KT + kt + 2) % ERING)
                            if kt == 7 and not end:
                                rows(gq + 1, ((j + 1) // NQC) % 2, (j + 1) % NQC)
                        act.wait_ge(s["av_mm"], gq * KT + KT + ERING)
                        act.wait_ge(s["ot_mm"], gq + 1)
                        nc.scalar.copy(o_s[:, j % 2, :], ps[:, AV + j % 2, 0:96]).then_inc(s["o_sb"], 1)

                with act.Fori(0, NH // 2 - 1) as m:
                    pair(m, False)
                pair(NH // 2 - 1, True)
                for c in range(B * NCH):
                    act.wait_ge(s["zt_mm"], c + 1)
                    if c >= 2:
                        act.wait_ge(s["z_mm"], c - 1)
                    nc.scalar.copy(z_t[:, c % 2, :], ps[:, c % 2, 0:CH]).then_inc(s["zt"], 1)

            @block.vector
            def _(dve):
                def write(b, mean, rstd):
                    return nc.vector.tensor_scalar(xg[:, b * S:(b + 1) * S], g["x"][:, b * S:(b + 1) * S],
                                                   mean, rstd, ALU.subtract, ALU.mult)
                norm_vector(nc, dve, s, g, write)
                for b in range(B):
                    for side in range(2):
                        for r in range(NCH):
                            n = (2 * b + side) * NCH + r
                            p0, p1, p2 = (part[:, side, i, r * CH:(r + 1) * CH] for i in range(3))
                            dve.wait_ge(s["part1"], n + 1)
                            nc.vector.scalar_tensor_tensor(rest[:, n % 2, :], ps[:, n % 2, 0:CH],
                                                           HD ** -0.5 if side == 0 else 1.0, p0,
                                                           ALU.mult, ALU.subtract).then_inc(s["part2"], 1)
                            dve.wait_ge(s["part2"], 2 * n + 1)
                            nc.vector.tensor_copy(p1, rest[:, n % 2, :]).then_inc(s["part2"], 1)
                            dve.wait_ge(s["part2"], 2 * n + 2)
                            nc.vector.tensor_tensor(p2, rest[:, n % 2, :], p1, ALU.subtract).then_inc(s["split"], 1)
                dve.sem_inc(s["max"], 2)
                dve.sem_inc(s["out"], 1)

                def reduce(ga, slot, kt):
                    dve.wait_ge(s["a_mm"], ga * KT + kt + 1)
                    nc.vector.tensor_reduce(mx[:, slot, kt // NQC, kt % NQC:kt % NQC + 1],
                                            ps[:, AB + kt % 2, 0:CH], AX.X, ALU.max).then_inc(s["max"], 1)
                    if kt == KT - 1:
                        dve.wait_ge(s["max"], ga * KT + KT + 2)
                        nc.vector.tensor_reduce(nm[:, slot, :], mx[:, slot, :, :], AX.X, ALU.max, negate=True) \
                            .then_inc(s["negmax"], 1)

                for ga in range(2):
                    for kt in range(KT):
                        reduce(ga, ga, kt)

                def normalise(at, chunk):
                    dve.wait_ge(s["ot_mm"], at + 1)
                    o4 = ps[0:96, MISC, 0:128].rearrange("p (j d) -> p j d", d=32)
                    nc.vector.reciprocal(rec[:, :], o4[:, :, HD]).then_inc(s["ochain"], 1)
                    dve.wait_ge(s["ochain"], at + 1)
                    nc.vector.tensor_tensor(
                        o_t[:, :, :, :].rearrange("p g j d -> p (g j d)")[:, bass.ds(at * (4 * HD), 4 * HD)]
                        .rearrange("p (j d) -> p j d", d=HD),
                        o4[:, :, 0:HD], rec[:, :].unsqueeze(2).to_broadcast([96, 4, HD]), ALU.mult) \
                        .then_inc(s["out"], 1)

                def pair(m, last):
                    for j in range(PAIR):
                        gq = m * PAIR + j
                        for kt in range(KT):
                            if not (last and j >= PAIR - 2):
                                if kt == 2:
                                    dve.wait_ge(s["nsplit"], gq + 1)
                                reduce(gq + 2, j % 2, kt)
                            if kt == 10:
                                normalise(gq, j)

                with dve.Fori(0, NH // 2 - 1) as m:
                    pair(m, False)
                pair(NH // 2 - 1, True)
                normalise(CHUNKS, 0)
                for c in range(B * NCH):
                    dve.wait_ge(s["z_mm"], c + 1)
                    xt = g["x"][:, c * CH:(c + 1) * CH]
                    nc.vector.tensor_tensor(xt, ps[:, 2 + c % 2, 0:CH], xt, ALU.add).then_inc(s["z_added"], 1)

            @block.tensor
            def _(pe):
                norm_tensor(nc, pe, s, g)
                for b in range(B):
                    pe.wait_ge(s["norm"], b + 1)
                    for side in range(2):
                        for r in range(NCH):
                            n = (2 * b + side) * NCH + r
                            if n >= 2:
                                pe.wait_ge(s["part2"], 2 * n - 3)
                            nc.tensor.matmul(ps[:, n % 2, 0:CH], g["wqk"][:, side, :],
                                             xg[:, b * S + r * CH:b * S + (r + 1) * CH],
                                             start=True, stop=True).then_inc(s["proj"], 1)
                for n in range(N // 128):
                    if n >= 2:
                        pe.wait_ge(s["v_all"], n - 1)
                    nc.tensor.matmul(ps[:, 2 + n % 2, 0:128], xg[:, n * 128:(n + 1) * 128], g["wv"][:, :],
                                     start=True, stop=True).then_inc(s["v_mm"], 1)
                pe.wait_ge(s["part2"], 2 * 2 * B * NCH)
                pe.wait_ge(s["v_all"], N // 128)
                pe.wait_ge(s["const"], 1)
                pe.sem_inc(s["av_mm"], ERING)

                def scores(step, bank, head_slot, c, kt):
                    pe.wait_ge(s["exp"], step + 2)
                    nc.tensor.matmul(ps[:, ST + bank, 0:QC], ks[:, head_slot, kt * 128:(kt + 1) * 128],
                                     qs[:, head_slot, c * QC:(c + 1) * QC], start=True, stop=True) \
                        .then_inc(s["st_mm"], 1)

                def by_query(ga, head_slot, c, u):
                    pe.wait_ge(s["max"], ga * KT + u + 1)
                    q0 = c * QC + (u // NQC) * 128
                    nc.tensor.matmul(ps[:, AB + u % 2, 0:CH], qs[0:KROWS, head_slot, q0:q0 + 128],
                                     ks[0:KROWS, head_slot, (u % NQC) * CH:(u % NQC + 1) * CH],
                                     start=True, stop=True).then_inc(s["a_mm"], 1)

                def rows(gr, slot):
                    pe.wait_ge(s["nsplit"], gr + 1)
                    for i in range(3):
                        last = nc.tensor.matmul(ps[KROWS:KROWS + MROWS, MISC, i * 128:(i + 1) * 128],
                                                nsp[:, slot, i, :], identb[:, :], start=True, stop=True,
                                                tile_position=(0, KROWS))
                    last.then_inc(s["rows_mm"], 1)

                pe.wait_ge(s["loaded0"], LOADS)
                for ga in range(2):
                    for u in range(KT):
                        by_query(ga, 0, ga, u)
                rows(0, 0)
                pe.wait_ge(s["rows"], 1)
                for kt in range(2):
                    scores(kt, kt, 0, 0, kt)

                def pair(m, last):
                    for j in range(PAIR):
                        gq = m * PAIR + j
                        end = last and j == PAIR - 1
                        if j % NQC == 0:
                            pe.wait_ge(s["v_slot"], m * 2 + (j // NQC + 1))
                        pe.wait_ge(s["o_sb"], gq + 1)
                        for kt in range(KT):
                            if kt + 2 < KT:
                                scores(gq * KT + (kt + 2), (kt + 2) % 3, (j // NQC) % 2, j % NQC, kt + 2)
                            elif not end:
                                if kt + 2 == KT:
                                    pe.wait_ge(s["rows"], gq + 2)
                                scores(gq * KT + (kt + 2), (kt + 2) % 3, ((j + 1) // NQC) % 2, (j + 1) % NQC,
                                       kt + 2 - KT)
                            if not (last and j >= PAIR - 2):
                                head, c = divmod(j + 2, NQC)
                                if c == 0 and kt == 0:
                                    pe.wait_ge(loaded[head % 2], m * LOADS + LOADS * (1 + head // 2))
                                by_query(gq + 2, head % 2, c, kt)
                            pe.wait_ge(s["exp"], gq * KT + (kt + 1 + ERING))
                            for i in range(4):
                                last_mm = nc.tensor.matmul(
                                    ps[32 * i:32 * i + 32, AV + j % 2, 0:96], v_s[:, (j // NQC) % 2, kt, :],
                                    e[:, (j * KT + kt) % ERING, 96 * i:96 * (i + 1)],
                                    start=(kt == 0), stop=(kt == KT - 1), tile_position=(0, 32 * i))
                            last_mm.then_inc(s["av_mm"], 1)
                            if kt == 5 and not end:
                                pe.wait_ge(s["out"], gq + 1)
                                rows(gq + 1, (j + 1) % 2)
                            if kt == 9:
                                if not end:
                                    pe.wait_ge(s["rows"], gq + 2)
                                turn_sums(gq, (j + 1) % 2)

                def turn_sums(at, slot):
                    pe.wait_ge(s["o_sb"], at + 2)
                    pe.wait_ge(s["out"], at + 1)
                    nc.tensor.transpose(ps[0:96, MISC, 0:128], o_s[:, slot, :], g["ident"][:, :]) \
                        .then_inc(s["ot_mm"], 1)

                with pe.Fori(0, NH // 2 - 1) as m:
                    pair(m, False)
                pair(NH // 2 - 1, True)
                turn_sums(CHUNKS, (CHUNKS - 1) % 2)
                pe.wait_ge(s["out"], CHUNKS + 2)
                pe.wait_ge(s["exp"], CHUNKS * KT + ERING)
                pe.wait_ge(s["o_sb"], CHUNKS + 2)
                for c in range(B * NCH):
                    b, r = divmod(c, NCH)
                    if c >= 2:
                        pe.wait_ge(s["zt"], c - 1)
                        pe.wait_ge(s["z_added"], c - 1)
                    pe.wait_ge(s["z_in"], c + 1)
                    for i in range(4):
                        last = nc.tensor.transpose(ps[:, c % 2, 96 * i:96 * (i + 1)], z_in[:, c % 2, i, :],
                                                   g["ident"][0:96, 0:96])
                    last.then_inc(s["zt_mm"], 1)
                    pe.wait_ge(s["zt"], c + 1)
                    nc.tensor.matmul(ps[:, 2 + c % 2, 0:CH], g["wo"][:, :], z_t[:, c % 2, :],
                                     start=True, stop=True).then_inc(s["z_mm"], 1)


CONSTS = [
    ("ident", [128, 128]), ("gavg", [128, 128]), ("base", [128, TILES * 2 * K2]),
    ("pw", [128, 128]), ("off_w", [128, 18]), ("off_b", [18, 1]), ("dw", [128, K2]),
    ("w1", [128, TG * RED]), ("b1", [TG * RED, 1]), ("gamma", [TG * RED, 1]), ("beta", [TG * RED, 1]),
    ("w2", [TG * RED, NTG, 128]), ("b2", [128, TAPS]),
    ("w_om", [128, K2, 27]), ("b_om", [27, 1]), ("w_dc", [128, K2, 128]), ("b_dc", [128, 1]),
    ("wqk", [128, 2, 128]), ("wv", [128, 128]), ("wo", [128, 128]),
]


def program(nc, x, consts, out, layers=(0, 1, 2, 3)):
    with ExitStack() as ctx:
        g = {name: ctx.enter_context(nc.sbuf_tensor(f"c_{name}", shape, F32)) for name, shape in CONSTS}
        for name, shape in (("bst", [128, B, NCH, 6]), ("mv", [128, B, 2]), ("msq", [128, B]), ("gm", [128, B, 2]),
                            ("var", [128, B]), ("std", [128, B]), ("rstd", [128, B]), ("eps", [128, 1])):
            g[name] = ctx.enter_context(nc.sbuf_tensor(f"n_{name}", shape, F32))
        g["x"] = ctx.enter_context(nc.sbuf_tensor("x_map", [128, N], F32))
        g["ps"] = ctx.enter_context(nc.psum_tensor("ps", [128, 8, BANK], F32))
        g["loaded"] = ctx.enter_context(nc.semaphore("inputs_loaded"))
        g["load_total"] = 16 * (B + len(CONSTS)) + 1

        with nc.Block() as block:
            @block.sync
            def _(sp):
                for b in range(B):
                    sp.dma_start(g["x"][:, b * S:(b + 1) * S], x[b, :, :]).then_inc(g["loaded"], 16)
                for name, shape in CONSTS:
                    sp.dma_start(g[name][:], consts[name]).then_inc(g["loaded"], 16)
                sp.wait_ge(g["loaded"], g["load_total"])

            @block.gpsimd
            def _(pool):
                nc.gpsimd.memset(g['eps'][:, :], 1e-5).then_inc(g["loaded"], 1)

        if 0 in layers:
            sampling_layer(nc, g, False)
        if 1 in layers:
            involution_layer(nc, g)
        if 2 in layers:
            sampling_layer(nc, g, True)
        if 3 in layers:
            attention_layer(nc, g, out)


def lay_out(i):
    f = np.float32
    pos = np.arange(S).reshape(TILES, 128).T
    tap = np.arange(K2)
    base = np.stack([pos[:, :, None] // W - 1 + tap // 3, pos[:, :, None] % W - 1 + tap % 3], -1)
    w2 = np.zeros((NTG * TG, RED, C), f)
    w2[:TAPS] = i["L1_conv_w2"].reshape(C, TAPS, RED).transpose(1, 2, 0)

    def rep(a):
        return np.concatenate([a.reshape(RED, -1)] * TG, 0)

    return {
        "ident": np.eye(128, dtype=f),
        "gavg": np.kron(np.eye(C // GROUP, dtype=f), np.full((GROUP, GROUP), 1.0 / GROUP, f)),
        "base": base.reshape(128, -1).astype(f),
        "pw": i["L0_conv_pw_w"].T, "off_w": i["L0_conv_off_w"].T, "off_b": i["L0_conv_off_b"][:, None],
        "dw": i["L0_conv_dw_w"].reshape(C, K2),
        "w1": rep(i["L1_conv_w1"]).T, "b1": rep(i["L1_conv_b1"]), "gamma": rep(i["L1_conv_gamma"]),
        "beta": rep(i["L1_conv_beta"]),
        "w2": w2.reshape(NTG, TG, RED, C).transpose(1, 2, 0, 3).reshape(TG * RED, NTG, C),
        "b2": i["L1_conv_b2"].reshape(C, TAPS),
        "w_om": i["L2_conv_w_om"].reshape(27, C, K2).transpose(1, 2, 0), "b_om": i["L2_conv_b_om"][:, None],
        "w_dc": i["L2_conv_w_dc"].reshape(C, C, K2).transpose(1, 2, 0), "b_dc": i["L2_conv_b_dc"][:, None],
        "wqk": np.stack([i["L3_conv_Wq"].T, i["L3_conv_Wk"].T], 1), "wv": i["L3_conv_Wv"].T,
        "wo": i["L3_conv_Wo"].T,
    }


def kernel(**inputs):
    import concourse.bacc as bacc
    from concourse.bass_utils import run_bass_kernel_spmd

    i = {k: np.asarray(v) for k, v in inputs.items()}
    arrays = {"x": i["x"].reshape(B, C, S)}
    arrays.update(lay_out(i))
    arrays = {k: np.ascontiguousarray(v) for k, v in arrays.items()}
    nc = bacc.Bacc("TRN2", target_bir_lowering=False, num_devices=1)
    aps = {k: nc.dram_tensor(f"in_{k}", v.shape, mybir.dt.from_np(v.dtype), kind="ExternalInput").ap()
           for k, v in arrays.items()}
    out = nc.dram_tensor("out", (B, C, S), F32, kind="ExternalOutput").ap()
    program(nc, aps["x"], aps, out)
    r = run_bass_kernel_spmd(nc, [{f"in_{k}": v for k, v in arrays.items()}], core_ids=[0])
    return r.results[0]["out"].reshape(B, C, H, W)
```

```python
from contextlib import ExitStack

import numpy as np

import concourse.bass as bass
from concourse import mybir

F32 = mybir.dt.float32
BF16 = mybir.dt.bfloat16
I32 = mybir.dt.int32
ALU = mybir.AluOpType
ACT = mybir.ActivationFunctionType
AX = mybir.AxisListType

B, C, H, W = 2, 128, 48, 48
S = H * W
N = B * S
GROUP = 4
ROWS = 8
CH = ROWS * W
NCH = S // CH
BANK = 512

K2 = 9
PW = 50
QT = 20
QN = QT * 128
GUARD = 64
TROWS = QN + GUARD
CORNERS = (0, 1, PW, PW + 1)
TILES = S // 128
SLOTS = 2

K7 = 7
TAPS = K7 * K7
RED = 32
IW = W + K7 - 1
IN = IW * IW
RP = 3 * RED
WQ = 4

HEADS, HD = 8, 16
NH = B * HEADS
KT = S // 128
QC = CH
NQC = S // QC
CHUNKS = NH * NQC
PAIR = 2 * NQC
Q_PARTS = (0, 0, 0, 1, 1, 2)
K_PARTS = (0, 1, 2, 0, 1, 0)
KROWS = len(Q_PARTS) * HD
MROWS = 3
ERING = 4


class Chain:

    def __init__(self, eng, sem):
        self.eng, self.sem, self.count, self.base = eng, sem, 0, 0

    def link(self, ins):
        self.count += 1
        ins.then_inc(self.sem, 1)
        self.eng.wait_ge(self.sem, self.base + self.count)


def semaphores(ctx, nc, prefix, names):
    return {n: ctx.enter_context(nc.semaphore(f"{prefix}_{n}")) for n in names.split()}


GN_SEMS = "stats means var std norm gchain gst "


def norm_vector(nc, dve, s, t, write):
    chain = Chain(dve, s["gchain"])
    for b in range(B):
        for q in range(NCH):
            last = nc.vector.bn_stats(t["bst"][:, b, q, :], t["x"][:, b * S + q * CH:b * S + (q + 1) * CH])
    chain.link(last)
    for b in range(B):
        last = nc.vector.bn_aggr(t["mv"][:, b, :], t["bst"][:, b, :, :].rearrange("p q e -> p (q e)"))
    chain.link(last)
    chain.link(nc.vector.tensor_tensor(t["msq"][:, :], t["mv"][:, :, 0], t["mv"][:, :, 0], ALU.mult))
    nc.vector.tensor_tensor(t["mv"][:, :, 1], t["mv"][:, :, 1], t["msq"][:, :], ALU.add).then_inc(s["stats"], 1)
    dve.wait_ge(s["means"], 1)
    chain.link(nc.vector.tensor_copy(t["gm"][:, :, :].rearrange("p b e -> p (b e)"), t["ps"][:, 0, 0:2 * B]))
    chain.link(nc.vector.tensor_tensor(t["msq"][:, :], t["gm"][:, :, 0], t["gm"][:, :, 0], ALU.mult))
    nc.vector.tensor_tensor(t["var"][:, :], t["gm"][:, :, 1], t["msq"][:, :], ALU.subtract).then_inc(s["var"], 1)
    dve.wait_ge(s["std"], 1)
    chain.link(nc.vector.reciprocal(t["rstd"][:, :], t["std"][:, :]))
    for b in range(B):
        write(b, t["gm"][:, b, 0:1], t["rstd"][:, b:b + 1]).then_inc(s["norm"], 1)


def norm_tensor(nc, pe, s, t):
    pe.wait_ge(s["stats"], 1)
    nc.tensor.matmul(t["ps"][:, 0, 0:2 * B], t["gavg"][:, :], t["mv"][:, :, :].rearrange("p b e -> p (b e)"),
                     start=True, stop=True).then_inc(s["means"], 1)


def norm_scalar(nc, act, s, t):
    act.wait_ge(s["var"], 1)
    nc.scalar.activation(t["std"][:, :], t["var"][:, :], ACT.Sqrt, bias=t["eps"][:, 0:1]).then_inc(s["std"], 1)


def window(img, b, r, ky, kx):
    at = (ROWS * r + ky) * PW + kx
    return img[:, b, at:at + ROWS * PW].rearrange("p (r w) -> p r w", w=PW)[:, :, 0:W]


SAMPLE_SEMS = GN_SEMS + ("zeroed pw_mm image off_mm offs tok_mm tok ot_mm mask chain index table0 table1 "
                         "gap gaps copied gather0 gather1 first_corner summed turned_mm turned out_mm added diag passed")


def sampling_layer(nc, g, modulated):
    R = 27 if modulated else 18
    with ExitStack() as ctx:
        def sb(name, shape, dt=F32):
            return ctx.enter_context(nc.sbuf_tensor(f"l{2 * modulated}_{name}", shape, dt))

        s = semaphores(ctx, nc, f"l{2 * modulated}", SAMPLE_SEMS)
        t = g
        ps = g["ps"]
        img = sb("img", [128, B, QN])
        offc = sb("offc", [R, N])
        tok = sb("tok", [128, B, QT, 128])
        yx = sb("yx", [128, TILES * K2, 2])
        fl = sb("fl", [128, TILES * K2, 2])
        ri = sb("ri", [128, TILES * K2, 2], I32)
        gt = sb("gt", [128, TILES * K2, 2])
        fr = sb("fr", [128, TILES * K2, 2])
        mk = sb("mk", [128, B, TILES * K2])
        qi = sb("qi", [128, TILES * K2])
        idx = sb("idx", [128, B * TILES * K2], I32)
        wts = sb("wts", [128, B * TILES * K2 * 4])
        idx_s = sb("idx_s", [128, SLOTS, K2], I32)
        wts_s = sb("wts_s", [128, SLOTS, K2 * 4])
        corner = sb("corner", [128, SLOTS, K2, 4 * 128])
        samp = sb("samp", [128, SLOTS, K2, 128])
        turned = sb("turned", [128, SLOTS, K2 * 128])
        if modulated:
            wk, offw, offb = g["w_dc"], g["w_om"], g["b_om"]
        else:
            wk = sb("wk", [128, K2, 128])
            offw, offb = g["off_w"], g["off_b"]
            xg = sb("xg", [128, N])
        gap = sb("gap", [GUARD, 4 * 128])
        table = [nc.dram_tensor(f"table{2 * modulated}_{b}", [TROWS, 4 * 128], F32).ap() for b in range(B)]
        gather = [s["gather0"], s["gather1"]]
        filled = [s["table0"], s["table1"]]

        with nc.Block() as block:

            @block.gpsimd
            def _(pool):
                nc.gpsimd.memset(gap[:, :], 0.0).then_inc(s["gap"], 1)
                nc.gpsimd.memset(img[:, :, :], 0.0).then_inc(s["zeroed"], 1)

                def tile(b, i, slot):
                    pool.wait_ge(s["summed"], 3 * i + 3)
                    nc.gpsimd.tensor_copy(idx_s[:, slot, :], idx[:, bass.ds(i * K2, K2)])
                    nc.gpsimd.tensor_copy(wts_s[:, slot, :], wts[:, bass.ds(i * K2 * 4, K2 * 4)]) \
                        .then_inc(s["copied"], 1)
                    pool.wait_ge(s["copied"], i + 1)
                    pool.sem_inc(s["passed"], 1)
                    for k in range(K2):
                        nc.gpsimd.indirect_dma_start(
                            corner[:, slot, k, :], None, table[b],
                            bass.IndirectOffsetOnAxis(ap=idx_s[:, slot, k:k + 1], axis=0),
                        ).then_inc(gather[slot], 16)

                for b in range(B):
                    pool.wait_ge(filled[b], 16 * len(CORNERS))
                    pool.wait_ge(s["index"], b + 1)
                    with pool.Fori(b * TILES // 2, (b + 1) * TILES // 2) as turn:
                        for slot in range(SLOTS):
                            tile(b, turn * SLOTS + slot, slot)

            @block.sync
            def _(sp):
                sp.wait_ge(s["gap"], 1)
                for b in range(B):
                    sp.dma_start(table[b][0:GUARD, :], gap[:, :]).then_inc(s["gaps"], 16)
                    sp.dma_start(table[b][QN:TROWS, :], gap[:, :]).then_inc(s["gaps"], 16)
                sp.wait_ge(s["gaps"], 16 * 2 * B)
                for b in range(B):
                    sp.wait_ge(s["tok"], (b + 1) * QT // 4)
                    for j, d in enumerate(CORNERS):
                        lo = GUARD - d
                        sp.dma_start(table[b][lo:lo + QN, j * 128:(j + 1) * 128]
                                     .rearrange("(t p) c -> p t c", p=128),
                                     tok[:, b, :, :]).then_inc(filled[b], 16)
                for b in range(B):
                    sp.wait_ge(filled[b], 16 * len(CORNERS))

            @block.scalar
            def _(act):
                norm_scalar(nc, act, s, t)
                act.wait_ge(s["zeroed"], 1)
                for b in range(B):
                    if not modulated:
                        for r in range(NCH):
                            n = b * NCH + r
                            act.wait_ge(s["pw_mm"], n + 1)
                            nc.scalar.copy(window(img, b, r, 1, 1),
                                           ps[:, n % 2, 0:CH].rearrange("p (r w) -> p r w", w=W)) \
                                .then_inc(s["image"], 1)
                    for r in range(NCH):
                        n = b * NCH + r
                        act.wait_ge(s["off_mm"], n + 1)
                        nc.scalar.activation(offc[:, n * CH:(n + 1) * CH], ps[0:R, 2 + n % 2, 0:CH],
                                             ACT.Identity, bias=offb[:, 0:1]).then_inc(s["offs"], 1)
                    for q in range(QT // 4):
                        n = b * (QT // 4) + q
                        act.wait_ge(s["tok_mm"], n + 1)
                        nc.scalar.copy(tok[:, b, 4 * q:4 * q + 4, :].rearrange("p t c -> p (t c)"),
                                       ps[:, 4 + n % 2, :]).then_inc(s["tok"], 1)
                    if modulated:
                        act.wait_ge(s["ot_mm"], b + 1)
                        nc.scalar.activation(
                            mk[:, b, :].rearrange("p (t k) -> p t k", k=K2),
                            ps[:, 6 + b, 0:TILES * R].rearrange("p (t r) -> p t r", r=R)[:, :, 2 * K2:R],
                            ACT.Sigmoid).then_inc(s["mask"], 1)

                act.sem_inc(s["turned"], SLOTS)
                with act.Fori(0, B * TILES // 2) as turn:
                    for slot in range(SLOTS):
                        i = turn * SLOTS + slot
                        act.wait_ge(gather[slot], turn * (16 * K2) + 16 * K2)
                        act.wait_ge(s["turned_mm"], i + 1)
                        for k in range(K2):
                            last = nc.scalar.activation(samp[:, slot, k, :], corner[:, slot, k, 0:128],
                                                        ACT.Copy, scale=wts_s[:, slot, 4 * k:4 * k + 1])
                        last.then_inc(s["first_corner"], 1)
                    for slot in range(SLOTS):
                        i = turn * SLOTS + slot
                        act.wait_ge(s["turned_mm"], i + 1 + SLOTS)
                        act.wait_ge(s["out_mm"], i + 1)
                        nc.scalar.copy(turned[:, slot, :].rearrange("p (a n) -> p a n", a=3),
                                       ps[:, 3 * slot:3 * slot + 3, 0:CH]).then_inc(s["turned"], 1)

            @block.vector
            def _(dve):
                if modulated:
                    dve.wait_ge(s["zeroed"], 1)

                    def write(b, mean, rstd):
                        return nc.vector.tensor_scalar(
                            img[:, b, PW + 1:PW + 1 + H * PW].rearrange("p (r w) -> p r w", w=PW)[:, :, 0:W],
                            g["x"][:, b * S:(b + 1) * S].rearrange("p (r w) -> p r w", w=W),
                            mean, rstd, ALU.subtract, ALU.mult)
                else:
                    def write(b, mean, rstd):
                        return nc.vector.tensor_scalar(xg[:, b * S:(b + 1) * S], g["x"][:, b * S:(b + 1) * S],
                                                       mean, rstd, ALU.subtract, ALU.mult)
                norm_vector(nc, dve, s, t, write)
                if not modulated:
                    for k in range(K2):
                        last = nc.vector.tensor_scalar(wk[:, k, :], g["ident"][:, :], g["dw"][:, k:k + 1], None,
                                                       ALU.mult)
                    last.then_inc(s["diag"], 1)
                chain = Chain(dve, s["chain"])
                for b in range(B):
                    dve.wait_ge(s["ot_mm"], b + 1)
                    if modulated:
                        dve.wait_ge(s["mask"], b + 1)
                    chain.link(nc.vector.tensor_tensor(
                        yx[:, :, :].rearrange("p (t k) e -> p t (k e)", k=K2),
                        ps[:, 6 + b, 0:TILES * R].rearrange("p (t r) -> p t r", r=R)[:, :, 0:2 * K2],
                        g["base"][:, :].rearrange("p (t r) -> p t r", r=2 * K2), ALU.add))
                    chain.link(nc.vector.tensor_scalar(yx[:, :, :], yx[:, :, :], -1.0, float(H),
                                                       ALU.max, ALU.min))
                    chain.link(nc.vector.tensor_copy(ri[:, :, :], yx[:, :, :]))
                    chain.link(nc.vector.tensor_copy(fl[:, :, :], ri[:, :, :]))
                    chain.link(nc.vector.tensor_tensor(gt[:, :, :], fl[:, :, :], yx[:, :, :], ALU.is_gt))
                    chain.link(nc.vector.tensor_tensor(fl[:, :, :], fl[:, :, :], gt[:, :, :], ALU.subtract))
                    chain.link(nc.vector.tensor_tensor(fr[:, :, :], yx[:, :, :], fl[:, :, :], ALU.subtract))
                    chain.link(nc.vector.tensor_scalar(gt[:, :, :], fr[:, :, :], -1.0, 1.0, ALU.mult, ALU.add))
                    if modulated:
                        chain.link(nc.vector.tensor_tensor(gt[:, :, 0], gt[:, :, 0], mk[:, b, :], ALU.mult))
                        chain.link(nc.vector.tensor_tensor(fr[:, :, 0], fr[:, :, 0], mk[:, b, :], ALU.mult))
                    w4 = wts[:, b * TILES * K2 * 4:(b + 1) * TILES * K2 * 4] \
                        .rearrange("p (n j) -> p n j", j=4)
                    for j, (wy, wx) in enumerate(((gt, gt), (gt, fr), (fr, gt), (fr, fr))):
                        nc.vector.tensor_tensor(w4[:, :, j], wy[:, :, 0], wx[:, :, 1], ALU.mult)
                    chain.link(nc.vector.scalar_tensor_tensor(qi[:, :], fl[:, :, 0], float(PW), fl[:, :, 1],
                                                              ALU.mult, ALU.add))
                    last = nc.vector.tensor_scalar(idx[:, b * TILES * K2:(b + 1) * TILES * K2], qi[:, :],
                                                   float(GUARD + PW + 1), None, ALU.add)
                    last.then_inc(s["index"], 1)
                    dve.wait_ge(s["index"], b + 1)

                dve.sem_inc(s["summed"], 3 * SLOTS)
                dve.sem_inc(s["added"], SLOTS)
                with dve.Fori(0, B * TILES // 2) as turn:
                    for slot in range(SLOTS):
                        i = turn * SLOTS + slot
                        dve.wait_ge(s["first_corner"], i + 1)
                        for j in range(1, 4):
                            for k in range(K2):
                                last = nc.vector.scalar_tensor_tensor(
                                    samp[:, slot, k, :], corner[:, slot, k, j * 128:(j + 1) * 128],
                                    wts_s[:, slot, 4 * k + j:4 * k + j + 1], samp[:, slot, k, :],
                                    ALU.mult, ALU.add)
                            last.then_inc(s["summed"], 1)
                            if j < 3:
                                dve.wait_ge(s["summed"], 3 * i + 3 * SLOTS + j)
                    for slot in range(SLOTS):
                        i = turn * SLOTS + slot
                        dve.wait_ge(s["out_mm"], i + 1 + SLOTS)
                        xt = g["x"][:, bass.ds(i * 128, 128)]
                        if modulated:
                            ins = nc.vector.scalar_tensor_tensor(xt, ps[:, 6 + slot, 0:128], g["b_dc"][:, 0:1], xt,
                                                                 ALU.add, ALU.add)
                        else:
                            ins = nc.vector.tensor_tensor(xt, ps[:, 6 + slot, 0:128], xt, ALU.add)
                        ins.then_inc(s["added"], 1)

            @block.tensor
            def _(pe):
                norm_tensor(nc, pe, s, t)
                for b in range(B):
                    pe.wait_ge(s["norm"], b + 1)
                    if not modulated:
                        for r in range(NCH):
                            n = b * NCH + r
                            if n >= 2:
                                pe.wait_ge(s["image"], n - 1)
                            nc.tensor.matmul(ps[:, n % 2, 0:CH], g["pw"][:, :], xg[:, n * CH:(n + 1) * CH],
                                             start=True, stop=True).then_inc(s["pw_mm"], 1)
                        pe.wait_ge(s["image"], (b + 1) * NCH)
                    for r in range(NCH):
                        n = b * NCH + r
                        if n >= 2:
                            pe.wait_ge(s["offs"], n - 1)
                        if modulated:
                            for k in range(K2):
                                last = nc.tensor.matmul(ps[0:R, 2 + n % 2, 0:CH], offw[:, k, :],
                                                        window(img, b, r, k // 3, k % 3),
                                                        start=(k == 0), stop=(k == K2 - 1))
                        else:
                            last = nc.tensor.matmul(ps[0:R, 2 + n % 2, 0:CH], offw[:, :],
                                                    window(img, b, r, 1, 1), start=True, stop=True)
                        last.then_inc(s["off_mm"], 1)
                    for q in range(QT // 4):
                        n = b * (QT // 4) + q
                        if n >= 2:
                            pe.wait_ge(s["tok"], n - 1)
                        for j in range(4):
                            at = (4 * q + j) * 128
                            last = nc.tensor.transpose(ps[:, 4 + n % 2, j * 128:(j + 1) * 128],
                                                       img[:, b, at:at + 128], g["ident"][:, :])
                        last.then_inc(s["tok_mm"], 1)
                    pe.wait_ge(s["offs"], (b + 1) * NCH)
                    for i in range(TILES):
                        at = b * S + i * 128
                        last = nc.tensor.transpose(ps[:, 6 + b, i * R:(i + 1) * R], offc[:, at:at + 128],
                                                   g["ident"][0:R, 0:R])
                    last.then_inc(s["ot_mm"], 1)

                pe.wait_ge(s["tok"], B * QT // 4)
                pe.wait_ge(s["index"], B)
                if not modulated:
                    pe.wait_ge(s["diag"], 1)
                pe.sem_inc(s["turned_mm"], SLOTS)
                pe.sem_inc(s["out_mm"], SLOTS)
                with pe.Fori(0, B * TILES // 2) as turn:
                    for slot in range(SLOTS):
                        i = turn * SLOTS + slot
                        pe.wait_ge(s["summed"], 3 * i + 3 * SLOTS + 3)
                        pe.wait_ge(s["turned"], i + 1)
                        for k in range(K2):
                            last = nc.tensor.transpose(ps[:, 3 * slot + k // 3, (k % 3) * 128:(k % 3 + 1) * 128],
                                                       samp[:, slot, k, :], g["ident"][:, :])
                        last.then_inc(s["turned_mm"], 1)
                        pe.wait_ge(s["turned"], i + 1 + SLOTS)
                        pe.wait_ge(s["added"], i + 1)
                        for k in range(K2):
                            last = nc.tensor.matmul(ps[:, 6 + slot, 0:128], wk[:, k, :],
                                                    turned[:, slot, k * 128:(k + 1) * 128],
                                                    start=(k == 0), stop=(k == K2 - 1))
                        last.then_inc(s["out_mm"], 1)


INV_SEMS = GN_SEMS + ("zeroed ones padded red_mm red rstats rvar rstd rnorm chain relu first rest second prepared "
                      "wgt_mm products dsum psum acc_mm added")


def involution_layer(nc, g):
    with ExitStack() as ctx:
        def sb(name, shape, dt=F32):
            return ctx.enter_context(nc.sbuf_tensor(f"l1_{name}", shape, dt))

        s = semaphores(ctx, nc, "l1", INV_SEMS)
        ps = g["ps"]
        xg = sb("xg", [128, N])
        pad = sb("pad", [128, B, IN])
        red = sb("red", [RP, N])
        rst = sb("rst", [RP, B * NCH * 6])
        rmv = sb("rmv", [RP, 2])
        rsd = sb("rsd", [RP, 1])
        rrs = sb("rrs", [RP, 1])
        scale = sb("scale", [RP, 1])
        shift = sb("shift", [RP, 1])
        relu = sb("relu", [RP, 2, CH])
        first = sb("first", [RP, 2, CH], BF16)
        rest = sb("rest", [RP, 2, CH])
        mov_a = sb("mov_a", [RP + 1, N], BF16)
        mov_b = sb("mov_b", [RP + 2, N], BF16)
        prod = sb("prod", [128, 2, K7, CH])
        RING = K7
        ACC = 7
        PAIRS = B * NCH // 2
        TP, RW = 2 * TAPS, 2 * K7

        with nc.Block() as block:

            @block.gpsimd
            def _(pool):
                nc.gpsimd.memset(pad[:, :, :], 0.0).then_inc(s["zeroed"], 1)
                with pool.Fori(0, PAIRS) as pair:
                    for row in range(RW):
                        q = row % 2

                        def add(i, j):
                            nc.gpsimd.tensor_tensor(prod[:, q, i, :], prod[:, q, i, :], prod[:, q, j, :],
                                                    ALU.add).then_inc(s["psum"], 1)

                        done = pair * TP + (row * K7 + RING)
                        pool.wait_ge(s["products"], done + 2)
                        add(0, 1)
                        pool.wait_ge(s["products"], done + 4)
                        add(2, 3)
                        pool.wait_ge(s["psum"], pair * (4 * RW) + (4 * row + 2))
                        add(0, 2)
                        pool.wait_ge(s["dsum"], pair * RW + (row + 1))
                        add(4, 6)

            @block.scalar
            def _(act):
                norm_scalar(nc, act, s, g)
                act.wait_ge(s["zeroed"], 1)
                for b in range(B):
                    act.wait_ge(s["norm"], b + 1)
                    nc.scalar.copy(pad[:, b, 3 * IW:3 * IW + H * IW].rearrange("p (r w) -> p r w", w=IW)[:, :, 3:3 + W],
                                   xg[:, b * S:(b + 1) * S].rearrange("p (r w) -> p r w", w=W)) \
                        .then_inc(s["padded"], 1)
                for n in range(B * NCH):
                    act.wait_ge(s["red_mm"], n + 1)
                    nc.scalar.activation(red[:, n * CH:(n + 1) * CH], ps[0:RP, n % 2, 0:CH], ACT.Identity,
                                         bias=g["b1"][:, 0:1]).then_inc(s["red"], 1)
                act.wait_ge(s["rvar"], 1)
                nc.scalar.activation(rsd[:, :], rmv[:, 1:2], ACT.Sqrt, bias=g["eps"][0:RP, 0:1]).then_inc(s["rstd"], 1)
                act.wait_ge(s["rnorm"], 1)
                for n in range(B * NCH + 1):
                    if n < B * NCH:
                        src = red[:, n * CH:(n + 1) * CH]
                        if n >= 2:
                            act.wait_ge(s["rest"], n - 1)
                        nc.scalar.activation(relu[:, n % 2, :], src, ACT.Relu, bias=shift[:, 0:1],
                                             scale=scale[:, 0:1])
                        nc.scalar.activation(first[:, n % 2, :], src, ACT.Relu, bias=shift[:, 0:1],
                                             scale=scale[:, 0:1]).then_inc(s["first"], 1)
                    if n:
                        m = n - 1
                        act.wait_ge(s["rest"], m + 1)
                        nc.scalar.copy(mov_b[RED:2 * RED, m * CH:(m + 1) * CH], rest[RED:2 * RED, m % 2, :])
                        nc.scalar.copy(mov_a[2 * RED:RP, m * CH:(m + 1) * CH], rest[2 * RED:RP, m % 2, :]) \
                            .then_inc(s["second"], 1)

            @block.vector
            def _(dve):
                def write(b, mean, rstd):
                    return nc.vector.tensor_scalar(xg[:, b * S:(b + 1) * S], g["x"][:, b * S:(b + 1) * S],
                                                   mean, rstd, ALU.subtract, ALU.mult)
                norm_vector(nc, dve, s, g, write)
                nc.vector.memset(mov_a[RP:RP + 1, :], 1.0)
                nc.vector.memset(mov_b[RP:RP + 2, :], 1.0).then_inc(s["ones"], 1)
                chain = Chain(dve, s["chain"])
                for n in range(B * NCH):
                    dve.wait_ge(s["red"], n + 1)
                    last = nc.vector.bn_stats(rst[:, n * 6:(n + 1) * 6], red[:, n * CH:(n + 1) * CH])
                chain.link(last)
                nc.vector.bn_aggr(rmv[:, :], rst[:, :]).then_inc(s["rvar"], 1)
                dve.wait_ge(s["rstd"], 1)
                chain.link(nc.vector.reciprocal(rrs[:, :], rsd[:, :]))
                chain.link(nc.vector.tensor_tensor(scale[:, :], rrs[:, :], g["gamma"][:, :], ALU.mult))
                chain.link(nc.vector.tensor_tensor(shift[:, :], rmv[:, 0:1], scale[:, :], ALU.mult))
                nc.vector.tensor_tensor(shift[:, :], g["beta"][:, :], shift[:, :], ALU.subtract).then_inc(s["rnorm"], 1)
                for n in range(B * NCH + 1):
                    if n < B * NCH:
                        at = slice(n * CH, (n + 1) * CH)
                        dve.wait_ge(s["first"], n + 1)
                        if n >= 2:
                            dve.wait_ge(s["prepared"], n - 1)
                        nc.vector.tensor_copy(mov_a[0:2 * RED, at], first[0:2 * RED, n % 2, :])
                        nc.vector.tensor_copy(mov_b[0:RED, at], first[0:RED, n % 2, :])
                        nc.vector.tensor_tensor(rest[:, n % 2, :], relu[:, n % 2, :], first[:, n % 2, :],
                                                ALU.subtract).then_inc(s["rest"], 1)
                    if n:
                        m = n - 1
                        at = slice(m * CH, (m + 1) * CH)
                        dve.wait_ge(s["second"], m + 1)
                        nc.vector.tensor_tensor(mov_b[2 * RED:RP, at], rest[2 * RED:RP, m % 2, :],
                                                mov_a[2 * RED:RP, at], ALU.subtract).then_inc(s["prepared"], 1)
                dve.wait_ge(s["padded"], B)
                dve.sem_inc(s["products"], RING)
                dve.sem_inc(s["added"], 1)
                flat = pad[:, :, :].rearrange("p b n -> p (b n)")

                def into_x(c):
                    xt = g["x"][:, bass.ds(c * CH, CH)]
                    nc.vector.tensor_tensor(xt, ps[:, ACC, 0:CH], xt, ALU.add).then_inc(s["added"], 1)

                def rows(pair, b, r2, first):
                    for row in range(RW):
                        half, ky = divmod(row, K7)
                        dve.wait_ge(s["acc_mm"], pair * RW + (row + 1))
                        for kx in range(K7):
                            dve.wait_ge(s["wgt_mm"], pair * TP + (row * K7 + kx + 1))
                            src = flat[:, bass.ds(b * IN + r2 * (2 * ROWS * IW) + (half * ROWS + ky) * IW,
                                                  ROWS * IW)] \
                                .rearrange("p (r w) -> p r w", w=IW)[:, :, kx:kx + W]
                            nc.vector.tensor_tensor(
                                prod[:, row % 2, kx, :].rearrange("p (r w) -> p r w", w=W),
                                ps[:, kx, 0:CH].rearrange("p (r w) -> p r w", w=W), src, ALU.mult) \
                                .then_inc(s["products"], 1)
                        dve.wait_ge(s["products"], pair * TP + (row * K7 + K7 - 1 + RING))
                        nc.vector.tensor_tensor(prod[:, row % 2, 4, :], prod[:, row % 2, 4, :],
                                                prod[:, row % 2, 5, :], ALU.add).then_inc(s["dsum"], 1)
                        if row == 1 and not first:
                            dve.wait_ge(s["acc_mm"], pair * RW + 2)
                            into_x(pair * 2 - 1)
                        if row == K7 + 1:
                            dve.wait_ge(s["acc_mm"], pair * RW + (K7 + 2))
                            into_x(pair * 2)

                rows(0, 0, 0, True)
                with dve.Fori(1, NCH // 2) as r2:
                    rows(r2, 0, r2, False)
                with dve.Fori(0, NCH // 2) as r2:
                    rows(r2 + NCH // 2, 1, r2, False)
                dve.wait_ge(s["acc_mm"], PAIRS * RW + 2)
                into_x(B * NCH - 1)

            @block.tensor
            def _(pe):
                norm_tensor(nc, pe, s, g)
                for n in range(B * NCH):
                    pe.wait_ge(s["norm"], n // NCH + 1)
                    if n >= 2:
                        pe.wait_ge(s["red"], n - 1)
                    nc.tensor.matmul(ps[0:RP, n % 2, 0:CH], g["w1"][:, :], xg[:, n * CH:(n + 1) * CH],
                                     start=True, stop=True).then_inc(s["red_mm"], 1)
                pe.wait_ge(s["red"], B * NCH)
                pe.wait_ge(s["ones"], 1)
                pe.wait_ge(s["prepared"], B * NCH)
                pe.sem_inc(s["acc_mm"], 2)

                def weights(pair, row, kx):
                    tap, k = row * K7 + kx, row * K7 % TAPS + kx
                    at = bass.ds(pair * (2 * CH) + (row // K7) * CH, CH)
                    pe.wait_ge(s["products"], pair * TP + (tap + 1))
                    nc.tensor.matmul(ps[:, kx, 0:CH], g["wgt_a"][:, k * 128:(k + 1) * 128], mov_a[:, at],
                                     start=True, stop=False)
                    nc.tensor.matmul(ps[:, kx, 0:CH], g["wgt_b"][:, k * 128:(k + 1) * 128], mov_b[:, at],
                                     start=False, stop=True).then_inc(s["wgt_mm"], 1)

                def add(pair, row):
                    pe.wait_ge(s["psum"], pair * (4 * RW) + (4 * row + 4))
                    if row % K7 == 0:
                        pe.wait_ge(s["added"], pair * 2 + (row // K7 + 1))
                    for j in (0, 4):
                        last = nc.tensor.matmul(ps[:, ACC, 0:CH], g["ident"][:, :], prod[:, row % 2, j, :],
                                                start=(row % K7 == 0 and j == 0),
                                                stop=(row % K7 == K7 - 1 and j == 4))
                    last.then_inc(s["acc_mm"], 1)

                def rows(pair, first):
                    for row in range(RW):
                        for kx in range(K7):
                            weights(pair, row, kx)
                            if kx == 1 and not (first and row < 2):
                                add(pair, row - 2)

                rows(0, True)
                with pe.Fori(1, PAIRS) as pair:
                    rows(pair, False)
                add(PAIRS, -2)
                add(PAIRS, -1)


ATT_SEMS = GN_SEMS + ("const proj part1 part2 split v_mm v_all stored loaded0 loaded1 v_slot st_mm exp av_mm "
                      "a_mm max negmax nsplit rows_mm rows o_sb ot_mm ochain out z_in zt_mm zt z_mm z_added saved "
                      "pchain passed")


def attention_layer(nc, g, out):
    with ExitStack() as ctx:
        def sb(name, shape, dt=F32):
            return ctx.enter_context(nc.sbuf_tensor(f"l3_{name}", shape, dt))

        s = semaphores(ctx, nc, "l3", ATT_SEMS)
        ps = g["ps"]
        xg = sb("xg", [128, N])
        part = sb("part", [128, 2, 3, S], BF16)
        rest = sb("rest", [128, 2, CH])
        v_all = sb("v_all", [128, NH, KT, HD])
        v_s = sb("v_s", [128, 2, KT, 32])
        qs = sb("qs", [KROWS + MROWS, 2, S], BF16)
        ks = sb("ks", [KROWS + MROWS, 2, S], BF16)
        e = sb("e", [128, ERING, QC])
        mx = sb("mx", [128, 2, 3, NQC])
        nm = sb("nm", [128, 2, 3])
        nr = sb("nr", [128, 2, 3])
        nsp = sb("nsp", [128, 2, 3, MROWS], BF16)
        identb = sb("identb", [128, 128], BF16)
        o_s = sb("o_s", [128, 2, 96])
        rec = sb("rec", [96, 4])
        o_t = sb("o_t", [96, 1 + CHUNKS, 4, HD])
        z_in = sb("z_in", [96, 2, 4, C])
        z_t = sb("z_t", [128, 2, CH])
        stack = nc.dram_tensor("qk_parts", [2 * 3 * B * 128, S], BF16).ap()
        ST, AB, AV, MISC = 0, 3, 5, 7
        loaded = [s["loaded0"], s["loaded1"]]
        LOADS = 16 * 2 * len(Q_PARTS)

        with nc.Block() as block:

            @block.sync
            def _(sp):
                for b in range(B):
                    for side in range(2):
                        sp.wait_ge(s["split"], (2 * b + side + 1) * NCH)
                        for p in range(3):
                            r0 = (side * 3 + p) * B * 128 + b * 128
                            sp.dma_start(stack[r0:r0 + 128, :], part[:, side, p, :]).then_inc(s["stored"], 16)
                sp.wait_ge(s["stored"], 16 * 3 * 2 * B)

                def load(n, slot):
                    for side, (tile, parts) in enumerate(((qs, Q_PARTS), (ks, K_PARTS))):
                        for i, p in enumerate(parts):
                            sp.dma_start(tile[HD * i:HD * (i + 1), slot, :],
                                         stack[bass.ds(n * HD + (side * 3 + p) * B * 128, HD), :]) \
                                .then_inc(loaded[slot], 16)

                load(0, 0)
                load(1, 1)
                with sp.Fori(0, NH // 2 - 1) as m:
                    for slot in range(2):
                        sp.wait_ge(s["st_mm"], m * (2 * NQC * KT) + (slot + 1) * NQC * KT)
                        load(m * 2 + (2 + slot), slot)
                for c in range(B * NCH):
                    sp.wait_ge(s["z_added"], c + 1)
                    b, r = divmod(c, NCH)
                    sp.dma_start(out[b, :, r * CH:(r + 1) * CH], g["x"][:, c * CH:(c + 1) * CH]).then_inc(s["saved"], 16)
                sp.wait_ge(s["saved"], 16 * B * NCH)

            @block.gpsimd
            def _(pool):
                chain = Chain(pool, s["pchain"])
                chain.link(nc.gpsimd.memset(v_s[:, :, :, HD:32], 0.0))
                chain.link(nc.gpsimd.memset(ks[KROWS:KROWS + MROWS, :, :], 1.0))
                chain.link(nc.gpsimd.memset(o_s[:, :, :], 1.0))
                chain.link(nc.gpsimd.tensor_copy(identb[:, :], g["ident"][:, :]))
                nc.gpsimd.memset(v_s[:, :, :, HD:HD + 1], 1.0).then_inc(s["const"], 1)
                pool.wait_ge(s["v_all"], N // 128)

                def take_v(n, slot):
                    nc.gpsimd.tensor_copy(
                        v_s[:, slot, :, 0:HD],
                        v_all[:, :, :, :].rearrange("p n t d -> p (n t d)")[:, bass.ds(n * (KT * HD), KT * HD)]
                        .rearrange("p (t d) -> p t d", d=HD)).then_inc(s["v_slot"], 1)

                take_v(0, 0)
                pool.wait_ge(s["const"], 1)
                def split_max(ga, slot):
                    pool.wait_ge(s["negmax"], ga + 1)
                    pool.sem_inc(s["passed"], 1)
                    n1, n2, n3 = (nsp[:, slot, :, i] for i in range(3))
                    chain.link(nc.gpsimd.tensor_copy(n1, nm[:, slot, :]))
                    chain.link(nc.gpsimd.tensor_tensor(nr[:, slot, :], nm[:, slot, :], n1, ALU.subtract))
                    pool.sem_inc(s["passed"], 1)
                    chain.link(nc.gpsimd.tensor_copy(n2, nr[:, slot, :]))
                    nc.gpsimd.tensor_tensor(n3, nr[:, slot, :], n2, ALU.subtract).then_inc(s["nsplit"], 1)

                split_max(0, 0)
                split_max(1, 1)

                def pair(m, last):
                    for j in range(PAIR):
                        gq = m * PAIR + j
                        if j % NQC == 1 and not (last and j > NQC):
                            n = m * 2 + j // NQC
                            pool.wait_ge(s["av_mm"], n * (NQC * KT) + ERING)
                            pool.sem_inc(s["passed"], 1)
                            take_v(n + 1, (j // NQC + 1) % 2)
                        if not (last and j >= PAIR - 2):
                            pool.wait_ge(s["rows_mm"], gq + 1)
                            split_max(gq + 2, j % 2)

                start, links = chain.count, 3 * PAIR
                with pool.Fori(0, NH // 2 - 1) as m:
                    chain.base = m * links
                    pair(m, False)
                assert chain.count == start + links
                chain.base, chain.count = 0, start + links * (NH // 2 - 1)
                pair(NH // 2 - 1, True)
                pool.wait_ge(s["out"], CHUNKS + 2)
                for c in range(B * NCH):
                    b, r = divmod(c, NCH)
                    if c >= 2:
                        pool.wait_ge(s["zt_mm"], c - 1)
                    g0 = 1 + b * HEADS * NQC + r
                    nc.gpsimd.tensor_copy(
                        z_in[:, c % 2, :, :].rearrange("p i (h d) -> p i h d", d=HD),
                        o_t[:, g0:g0 + (HEADS - 1) * NQC + 1:NQC, :, :].rearrange("p h i d -> p i h d")) \
                        .then_inc(s["z_in"], 1)

            @block.scalar
            def _(act):
                norm_scalar(nc, act, s, g)
                for b in range(B):
                    for side in range(2):
                        for r in range(NCH):
                            n = (2 * b + side) * NCH + r
                            act.wait_ge(s["proj"], n + 1)
                            if b and r == 0:
                                act.wait_ge(s["stored"], 16 * 3 * 2 * b)
                            nc.scalar.activation(part[:, side, 0, r * CH:(r + 1) * CH], ps[:, n % 2, 0:CH],
                                                 ACT.Copy, scale=HD ** -0.5 if side == 0 else 1.0) \
                                .then_inc(s["part1"], 1)
                for n in range(N // 128):
                    b, t = divmod(n, TILES)
                    act.wait_ge(s["v_mm"], n + 1)
                    nc.scalar.copy(v_all[:, b * HEADS:(b + 1) * HEADS, t, :],
                                   ps[:, 2 + n % 2, 0:128].rearrange("p (h d) -> p h d", d=HD)) \
                        .then_inc(s["v_all"], 1)
                act.wait_ge(s["const"], 1)
                act.sem_inc(s["exp"], ERING)
                act.sem_inc(s["o_sb"], 2)

                def exp(step, bank, slot):
                    act.wait_ge(s["st_mm"], step + 1)
                    act.wait_ge(s["av_mm"], step + 1)
                    nc.scalar.activation(e[:, slot, :], ps[:, ST + bank, 0:QC], ACT.Exp).then_inc(s["exp"], 1)

                def rows(gr, head_slot, c):
                    act.wait_ge(s["rows_mm"], gr + 1)
                    nc.scalar.copy(qs[KROWS:KROWS + MROWS, head_slot, c * QC:(c + 1) * QC],
                                   ps[KROWS:KROWS + MROWS, MISC, 0:QC]).then_inc(s["rows"], 1)

                rows(0, 0, 0)
                for kt in range(2):
                    exp(kt, kt, kt)

                def pair(m, last):
                    for j in range(PAIR):
                        gq = m * PAIR + j
                        end = last and j == PAIR - 1
                        for kt in range(KT):
                            if not (end and kt + 2 >= KT):
                                exp(gq * KT + (kt + 2), (kt + 2) % 3, (j * KT + kt + 2) % ERING)
                            if kt == 7 and not end:
                                rows(gq + 1, ((j + 1) // NQC) % 2, (j + 1) % NQC)
                        act.wait_ge(s["av_mm"], gq * KT + KT + ERING)
                        act.wait_ge(s["ot_mm"], gq + 1)
                        nc.scalar.copy(o_s[:, j % 2, :], ps[:, AV + j % 2, 0:96]).then_inc(s["o_sb"], 1)

                with act.Fori(0, NH // 2 - 1) as m:
                    pair(m, False)
                pair(NH // 2 - 1, True)
                for c in range(B * NCH):
                    act.wait_ge(s["zt_mm"], c + 1)
                    if c >= 2:
                        act.wait_ge(s["z_mm"], c - 1)
                    nc.scalar.copy(z_t[:, c % 2, :], ps[:, c % 2, 0:CH]).then_inc(s["zt"], 1)

            @block.vector
            def _(dve):
                def write(b, mean, rstd):
                    return nc.vector.tensor_scalar(xg[:, b * S:(b + 1) * S], g["x"][:, b * S:(b + 1) * S],
                                                   mean, rstd, ALU.subtract, ALU.mult)
                norm_vector(nc, dve, s, g, write)
                for b in range(B):
                    for side in range(2):
                        for r in range(NCH):
                            n = (2 * b + side) * NCH + r
                            p0, p1, p2 = (part[:, side, i, r * CH:(r + 1) * CH] for i in range(3))
                            dve.wait_ge(s["part1"], n + 1)
                            nc.vector.scalar_tensor_tensor(rest[:, n % 2, :], ps[:, n % 2, 0:CH],
                                                           HD ** -0.5 if side == 0 else 1.0, p0,
                                                           ALU.mult, ALU.subtract).then_inc(s["part2"], 1)
                            dve.wait_ge(s["part2"], 2 * n + 1)
                            nc.vector.tensor_copy(p1, rest[:, n % 2, :]).then_inc(s["part2"], 1)
                            dve.wait_ge(s["part2"], 2 * n + 2)
                            nc.vector.tensor_tensor(p2, rest[:, n % 2, :], p1, ALU.subtract).then_inc(s["split"], 1)
                dve.sem_inc(s["max"], 2)
                dve.sem_inc(s["out"], 1)

                def reduce(ga, slot, kt):
                    dve.wait_ge(s["a_mm"], ga * KT + kt + 1)
                    nc.vector.tensor_reduce(mx[:, slot, kt // NQC, kt % NQC:kt % NQC + 1],
                                            ps[:, AB + kt % 2, 0:CH], AX.X, ALU.max).then_inc(s["max"], 1)
                    if kt == KT - 1:
                        dve.wait_ge(s["max"], ga * KT + KT + 2)
                        nc.vector.tensor_reduce(nm[:, slot, :], mx[:, slot, :, :], AX.X, ALU.max, negate=True) \
                            .then_inc(s["negmax"], 1)

                for ga in range(2):
                    for kt in range(KT):
                        reduce(ga, ga, kt)

                def normalise(at, chunk):
                    dve.wait_ge(s["ot_mm"], at + 1)
                    o4 = ps[0:96, MISC, 0:128].rearrange("p (j d) -> p j d", d=32)
                    nc.vector.reciprocal(rec[:, :], o4[:, :, HD]).then_inc(s["ochain"], 1)
                    dve.wait_ge(s["ochain"], at + 1)
                    nc.vector.tensor_tensor(
                        o_t[:, :, :, :].rearrange("p g j d -> p (g j d)")[:, bass.ds(at * (4 * HD), 4 * HD)]
                        .rearrange("p (j d) -> p j d", d=HD),
                        o4[:, :, 0:HD], rec[:, :].unsqueeze(2).to_broadcast([96, 4, HD]), ALU.mult) \
                        .then_inc(s["out"], 1)

                def pair(m, last):
                    for j in range(PAIR):
                        gq = m * PAIR + j
                        for kt in range(KT):
                            if not (last and j >= PAIR - 2):
                                if kt == 2:
                                    dve.wait_ge(s["nsplit"], gq + 1)
                                reduce(gq + 2, j % 2, kt)
                            if kt == 10:
                                normalise(gq, j)

                with dve.Fori(0, NH // 2 - 1) as m:
                    pair(m, False)
                pair(NH // 2 - 1, True)
                normalise(CHUNKS, 0)
                for c in range(B * NCH):
                    dve.wait_ge(s["z_mm"], c + 1)
                    xt = g["x"][:, c * CH:(c + 1) * CH]
                    nc.vector.tensor_tensor(xt, ps[:, 2 + c % 2, 0:CH], xt, ALU.add).then_inc(s["z_added"], 1)

            @block.tensor
            def _(pe):
                norm_tensor(nc, pe, s, g)
                for b in range(B):
                    pe.wait_ge(s["norm"], b + 1)
                    for side in range(2):
                        for r in range(NCH):
                            n = (2 * b + side) * NCH + r
                            if n >= 2:
                                pe.wait_ge(s["part2"], 2 * n - 3)
                            nc.tensor.matmul(ps[:, n % 2, 0:CH], g["wqk"][:, side, :],
                                             xg[:, b * S + r * CH:b * S + (r + 1) * CH],
                                             start=True, stop=True).then_inc(s["proj"], 1)
                for n in range(N // 128):
                    if n >= 2:
                        pe.wait_ge(s["v_all"], n - 1)
                    nc.tensor.matmul(ps[:, 2 + n % 2, 0:128], xg[:, n * 128:(n + 1) * 128], g["wv"][:, :],
                                     start=True, stop=True).then_inc(s["v_mm"], 1)
                pe.wait_ge(s["part2"], 2 * 2 * B * NCH)
                pe.wait_ge(s["v_all"], N // 128)
                pe.wait_ge(s["const"], 1)
                pe.sem_inc(s["av_mm"], ERING)

                def scores(step, bank, head_slot, c, kt):
                    pe.wait_ge(s["exp"], step + 2)
                    nc.tensor.matmul(ps[:, ST + bank, 0:QC], ks[:, head_slot, kt * 128:(kt + 1) * 128],
                                     qs[:, head_slot, c * QC:(c + 1) * QC], start=True, stop=True) \
                        .then_inc(s["st_mm"], 1)

                def by_query(ga, head_slot, c, u):
                    pe.wait_ge(s["max"], ga * KT + u + 1)
                    q0 = c * QC + (u // NQC) * 128
                    nc.tensor.matmul(ps[:, AB + u % 2, 0:CH], qs[0:KROWS, head_slot, q0:q0 + 128],
                                     ks[0:KROWS, head_slot, (u % NQC) * CH:(u % NQC + 1) * CH],
                                     start=True, stop=True).then_inc(s["a_mm"], 1)

                def rows(gr, slot):
                    pe.wait_ge(s["nsplit"], gr + 1)
                    for i in range(3):
                        last = nc.tensor.matmul(ps[KROWS:KROWS + MROWS, MISC, i * 128:(i + 1) * 128],
                                                nsp[:, slot, i, :], identb[:, :], start=True, stop=True,
                                                tile_position=(0, KROWS))
                    last.then_inc(s["rows_mm"], 1)

                pe.wait_ge(s["loaded0"], LOADS)
                for ga in range(2):
                    for u in range(KT):
                        by_query(ga, 0, ga, u)
                rows(0, 0)
                pe.wait_ge(s["rows"], 1)
                for kt in range(2):
                    scores(kt, kt, 0, 0, kt)

                def pair(m, last):
                    for j in range(PAIR):
                        gq = m * PAIR + j
                        end = last and j == PAIR - 1
                        if j % NQC == 0:
                            pe.wait_ge(s["v_slot"], m * 2 + (j // NQC + 1))
                        pe.wait_ge(s["o_sb"], gq + 1)
                        for kt in range(KT):
                            if kt + 2 < KT:
                                scores(gq * KT + (kt + 2), (kt + 2) % 3, (j // NQC) % 2, j % NQC, kt + 2)
                            elif not end:
                                if kt + 2 == KT:
                                    pe.wait_ge(s["rows"], gq + 2)
                                scores(gq * KT + (kt + 2), (kt + 2) % 3, ((j + 1) // NQC) % 2, (j + 1) % NQC,
                                       kt + 2 - KT)
                            if not (last and j >= PAIR - 2):
                                head, c = divmod(j + 2, NQC)
                                if c == 0 and kt == 0:
                                    pe.wait_ge(loaded[head % 2], m * LOADS + LOADS * (1 + head // 2))
                                by_query(gq + 2, head % 2, c, kt)
                            pe.wait_ge(s["exp"], gq * KT + (kt + 1 + ERING))
                            for i in range(4):
                                last_mm = nc.tensor.matmul(
                                    ps[32 * i:32 * i + 32, AV + j % 2, 0:96], v_s[:, (j // NQC) % 2, kt, :],
                                    e[:, (j * KT + kt) % ERING, 96 * i:96 * (i + 1)],
                                    start=(kt == 0), stop=(kt == KT - 1), tile_position=(0, 32 * i))
                            last_mm.then_inc(s["av_mm"], 1)
                            if kt == 5 and not end:
                                pe.wait_ge(s["out"], gq + 1)
                                rows(gq + 1, (j + 1) % 2)
                            if kt == 9:
                                if not end:
                                    pe.wait_ge(s["rows"], gq + 2)
                                turn_sums(gq, (j + 1) % 2)

                def turn_sums(at, slot):
                    pe.wait_ge(s["o_sb"], at + 2)
                    pe.wait_ge(s["out"], at + 1)
                    nc.tensor.transpose(ps[0:96, MISC, 0:128], o_s[:, slot, :], g["ident"][:, :]) \
                        .then_inc(s["ot_mm"], 1)

                with pe.Fori(0, NH // 2 - 1) as m:
                    pair(m, False)
                pair(NH // 2 - 1, True)
                turn_sums(CHUNKS, (CHUNKS - 1) % 2)
                pe.wait_ge(s["out"], CHUNKS + 2)
                pe.wait_ge(s["exp"], CHUNKS * KT + ERING)
                pe.wait_ge(s["o_sb"], CHUNKS + 2)
                for c in range(B * NCH):
                    b, r = divmod(c, NCH)
                    if c >= 2:
                        pe.wait_ge(s["zt"], c - 1)
                        pe.wait_ge(s["z_added"], c - 1)
                    pe.wait_ge(s["z_in"], c + 1)
                    for i in range(4):
                        last = nc.tensor.transpose(ps[:, c % 2, 96 * i:96 * (i + 1)], z_in[:, c % 2, i, :],
                                                   g["ident"][0:96, 0:96])
                    last.then_inc(s["zt_mm"], 1)
                    pe.wait_ge(s["zt"], c + 1)
                    nc.tensor.matmul(ps[:, 2 + c % 2, 0:CH], g["wo"][:, :], z_t[:, c % 2, :],
                                     start=True, stop=True).then_inc(s["z_mm"], 1)


CONSTS = [
    ("ident", [128, 128]), ("gavg", [128, 128]), ("base", [128, TILES * 2 * K2]),
    ("pw", [128, 128]), ("off_w", [128, 18]), ("off_b", [18, 1]), ("dw", [128, K2]),
    ("w1", [128, RP]), ("b1", [RP, 1]), ("gamma", [RP, 1]), ("beta", [RP, 1]),
    ("w2", [WQ * RED, TAPS * C // WQ]), ("b2", [TAPS, C]),
    ("w_om", [128, K2, 27]), ("b_om", [27, 1]), ("w_dc", [128, K2, 128]), ("b_dc", [128, 1]),
    ("wqk", [128, 2, 128]), ("wv", [128, 128]), ("wo", [128, 128]),
]


def split_involution_weights(nc, g, ctx):
    M = TAPS * C // WQ
    g["wgt_a"] = ctx.enter_context(nc.sbuf_tensor("wgt_a", [RP + 1, TAPS * C], BF16))
    g["wgt_b"] = ctx.enter_context(nc.sbuf_tensor("wgt_b", [RP + 2, TAPS * C], BF16))
    with ExitStack() as tmp:
        s = semaphores(tmp, nc, "ws", "chain stacked")
        wp = [tmp.enter_context(nc.sbuf_tensor(f"wp{i}", [WQ * RED, M], BF16)) for i in range(3)]
        bp = [tmp.enter_context(nc.sbuf_tensor(f"bp{i}", [TAPS, C], BF16)) for i in range(3)]
        wr = tmp.enter_context(nc.sbuf_tensor("wr", [WQ * RED, M], F32))
        br = tmp.enter_context(nc.sbuf_tensor("br", [TAPS, C], F32))
        with nc.Block() as block:
            @block.vector
            def _(dve):
                chain = Chain(dve, s["chain"])
                for full, p, rest in ((g["w2"], wp, wr), (g["b2"], bp, br)):
                    chain.link(nc.vector.tensor_copy(p[0][:, :], full[:, :]))
                    chain.link(nc.vector.tensor_tensor(rest[:, :], full[:, :], p[0][:, :], ALU.subtract))
                    chain.link(nc.vector.tensor_copy(p[1][:, :], rest[:, :]))
                    chain.link(nc.vector.tensor_tensor(p[2][:, :], rest[:, :], p[1][:, :], ALU.subtract))

            @block.sync
            def _(sp):
                sp.wait_ge(s["chain"], 8)
                total = 0
                for dst, parts in ((g["wgt_a"], (0, 1, 0)), (g["wgt_b"], (2, 1, 0))):
                    for j, p in enumerate(parts):
                        for q in range(WQ):
                            sp.dma_start(dst[RED * j:RED * (j + 1), q * M:(q + 1) * M],
                                         wp[p][RED * q:RED * (q + 1), :]).then_inc(s["stacked"], 16)
                            total += 16
                for dst, row, p in ((g["wgt_a"], RP, 0), (g["wgt_b"], RP, 1), (g["wgt_b"], RP + 1, 2)):
                    sp.dma_start(dst[row:row + 1, :].rearrange("o (k c) -> o k c", c=C), bp[p][:, :])\
                        .then_inc(s["stacked"], 16)
                    total += 16
                sp.wait_ge(s["stacked"], total)


def program(nc, x, consts, out, layers=(0, 1, 2, 3)):
    with ExitStack() as ctx:
        g = {name: ctx.enter_context(nc.sbuf_tensor(f"c_{name}", shape, F32)) for name, shape in CONSTS}
        for name, shape in (("bst", [128, B, NCH, 6]), ("mv", [128, B, 2]), ("msq", [128, B]), ("gm", [128, B, 2]),
                            ("var", [128, B]), ("std", [128, B]), ("rstd", [128, B]), ("eps", [128, 1])):
            g[name] = ctx.enter_context(nc.sbuf_tensor(f"n_{name}", shape, F32))
        g["x"] = ctx.enter_context(nc.sbuf_tensor("x_map", [128, N], F32))
        g["ps"] = ctx.enter_context(nc.psum_tensor("ps", [128, 8, BANK], F32))
        g["loaded"] = ctx.enter_context(nc.semaphore("inputs_loaded"))
        g["load_total"] = 16 * (B + len(CONSTS)) + 1

        with nc.Block() as block:
            @block.sync
            def _(sp):
                for b in range(B):
                    sp.dma_start(g["x"][:, b * S:(b + 1) * S], x[b, :, :]).then_inc(g["loaded"], 16)
                for name, shape in CONSTS:
                    sp.dma_start(g[name][:], consts[name]).then_inc(g["loaded"], 16)
                sp.wait_ge(g["loaded"], g["load_total"])

            @block.gpsimd
            def _(pool):
                nc.gpsimd.memset(g['eps'][:, :], 1e-5).then_inc(g["loaded"], 1)

        if 0 in layers:
            sampling_layer(nc, g, False)
        if 1 in layers:
            with ExitStack() as held:
                split_involution_weights(nc, g, held)
                involution_layer(nc, g)
        if 2 in layers:
            sampling_layer(nc, g, True)
        if 3 in layers:
            attention_layer(nc, g, out)


def lay_out(i):
    f = np.float32
    pos = np.arange(S).reshape(TILES, 128).T
    tap = np.arange(K2)
    base = np.stack([pos[:, :, None] // W - 1 + tap // 3, pos[:, :, None] % W - 1 + tap % 3], -1)
    w2 = i["L1_conv_w2"].reshape(C, TAPS, RED).transpose(2, 1, 0).reshape(RED, WQ, TAPS * C // WQ)

    def rep(a):
        return np.concatenate([a.reshape(RED, -1)] * 3, 0)

    return {
        "ident": np.eye(128, dtype=f),
        "gavg": np.kron(np.eye(C // GROUP, dtype=f), np.full((GROUP, GROUP), 1.0 / GROUP, f)),
        "base": base.reshape(128, -1).astype(f),
        "pw": i["L0_conv_pw_w"].T, "off_w": i["L0_conv_off_w"].T, "off_b": i["L0_conv_off_b"][:, None],
        "dw": i["L0_conv_dw_w"].reshape(C, K2),
        "w1": rep(i["L1_conv_w1"]).T, "b1": rep(i["L1_conv_b1"]), "gamma": rep(i["L1_conv_gamma"]),
        "beta": rep(i["L1_conv_beta"]),
        "w2": w2.transpose(1, 0, 2).reshape(WQ * RED, -1), "b2": i["L1_conv_b2"].reshape(C, TAPS).T,
        "w_om": i["L2_conv_w_om"].reshape(27, C, K2).transpose(1, 2, 0), "b_om": i["L2_conv_b_om"][:, None],
        "w_dc": i["L2_conv_w_dc"].reshape(C, C, K2).transpose(1, 2, 0), "b_dc": i["L2_conv_b_dc"][:, None],
        "wqk": np.stack([i["L3_conv_Wq"].T, i["L3_conv_Wk"].T], 1), "wv": i["L3_conv_Wv"].T,
        "wo": i["L3_conv_Wo"].T,
    }


def kernel(**inputs):
    import concourse.bacc as bacc
    from concourse.bass_utils import run_bass_kernel_spmd

    i = {k: np.asarray(v) for k, v in inputs.items()}
    arrays = {"x": i["x"].reshape(B, C, S)}
    arrays.update(lay_out(i))
    arrays = {k: np.ascontiguousarray(v) for k, v in arrays.items()}
    nc = bacc.Bacc("TRN2", target_bir_lowering=False, num_devices=1)
    aps = {k: nc.dram_tensor(f"in_{k}", v.shape, mybir.dt.from_np(v.dtype), kind="ExternalInput").ap()
           for k, v in arrays.items()}
    out = nc.dram_tensor("out", (B, C, S), F32, kind="ExternalOutput").ap()
    program(nc, aps["x"], aps, out)
    r = run_bass_kernel_spmd(nc, [{f"in_{k}": v for k, v in arrays.items()}], core_ids=[0])
    return r.results[0]["out"].reshape(B, C, H, W)
```

```python
from contextlib import ExitStack

import numpy as np

import concourse.bass as bass
from concourse import mybir

F32 = mybir.dt.float32
BF16 = mybir.dt.bfloat16
I32 = mybir.dt.int32
ALU = mybir.AluOpType
ACT = mybir.ActivationFunctionType
AX = mybir.AxisListType

B, C, H, W = 2, 128, 48, 48
S = H * W
N = B * S
GROUP = 4
ROWS = 8
CH = ROWS * W
NCH = S // CH
BANK = 512

K2 = 9
PW = 50
QT = 20
QN = QT * 128
GUARD = 64
TROWS = QN + GUARD
CORNERS = (0, 1, PW, PW + 1)
TILES = S // 128
PARTS = 2
SLOTS = 2
GROUPS = 3
GK = K2 // GROUPS
RO = 32
OT = 3
ROUNDS = NCH // OT
RT = TILES // ROUNDS

K7 = 7
TAPS = K7 * K7
RED = 32
IW = W + K7 - 1
IN = IW * IW
RP = 3 * RED
WQ = 4

HEADS, HD = 8, 16
NH = B * HEADS
KT = S // 128
QC = CH
NQC = S // QC
CHUNKS = NH * NQC
CT = 4
AHEAD = CT + 1
Q_PARTS = (0, 0, 0, 1, 1, 2)
K_PARTS = (0, 1, 2, 0, 1, 0)
KROWS = len(Q_PARTS) * HD
MROWS = 3
ERING = 3


class Chain:

    def __init__(self, eng, sem):
        self.eng, self.sem, self.count, self.base = eng, sem, 0, 0

    def link(self, ins):
        self.count += 1
        ins.then_inc(self.sem, 1)
        self.eng.wait_ge(self.sem, self.base + self.count)


def semaphores(ctx, nc, prefix, names):
    return {n: ctx.enter_context(nc.semaphore(f"{prefix}_{n}")) for n in names.split()}


GN_SEMS = "stats means var std norm gchain "


def norm_vector(nc, dve, s, t, write, stats=None, loaded=None):
    chain = Chain(dve, s["gchain"])
    if stats is None:
        stats = NCH
        for b in range(B):
            if loaded:
                dve.wait_ge(loaded[b], 16)
            for q in range(NCH):
                last = nc.vector.bn_stats(t["bst"][:, b, q, :], t["x"][:, b * S + q * CH:b * S + (q + 1) * CH])
        chain.link(last)
    for b in range(B):
        last = nc.vector.bn_aggr(t["mv"][:, b, :], t["bst"][:, b, 0:stats, :].rearrange("p q e -> p (q e)"))
    chain.link(last)
    chain.link(nc.vector.tensor_tensor(t["msq"][:, :], t["mv"][:, :, 0], t["mv"][:, :, 0], ALU.mult))
    nc.vector.tensor_tensor(t["mv"][:, :, 1], t["mv"][:, :, 1], t["msq"][:, :], ALU.add).then_inc(s["stats"], 1)
    dve.wait_ge(s["means"], 1)
    chain.link(nc.vector.tensor_copy(t["gm"][:, :, :].rearrange("p b e -> p (b e)"), t["ps"][:, 0, 0:2 * B]))
    chain.link(nc.vector.tensor_tensor(t["msq"][:, :], t["gm"][:, :, 0], t["gm"][:, :, 0], ALU.mult))
    nc.vector.tensor_tensor(t["var"][:, :], t["gm"][:, :, 1], t["msq"][:, :], ALU.subtract).then_inc(s["var"], 1)
    dve.wait_ge(s["std"], 1)
    chain.link(nc.vector.reciprocal(t["rstd"][:, :], t["std"][:, :]))
    for b in range(B):
        write(b, t["gm"][:, b, 0:1], t["rstd"][:, b:b + 1]).then_inc(s["norm"], 1)


def norm_tensor(nc, pe, s, t):
    pe.wait_ge(s["stats"], 1)
    nc.tensor.matmul(t["ps"][:, 0, 0:2 * B], t["gavg"][:, :], t["mv"][:, :, :].rearrange("p b e -> p (b e)"),
                     start=True, stop=True).then_inc(s["means"], 1)


def norm_scalar(nc, act, s, t):
    act.wait_ge(s["var"], 1)
    nc.scalar.activation(t["std"][:, :], t["var"][:, :], ACT.Sqrt, bias=t["eps"][:, 0:1]).then_inc(s["std"], 1)


def window(img, b, r, ky, kx):
    at = (ROWS * r + ky) * PW + kx
    return img[:, b, at:at + ROWS * PW].rearrange("p (r w) -> p r w", w=PW)[:, :, 0:W]


SAMPLE_SEMS = GN_SEMS + ("zeroed pw_mm image off_mm offs tok_mm tok ot_mm mask chain index table0 table1 "
                         "gap gaps copied gather00 gather01 gather02 gather10 gather11 gather12 first_corner "
                         "weighed summed turned_mm turned out_mm added diag passed")


def sampling_layer(nc, g, modulated):
    TURNS = B * TILES // SLOTS
    with ExitStack() as ctx:
        def sb(name, shape, dt=F32):
            return ctx.enter_context(nc.sbuf_tensor(f"l{2 * modulated}_{name}", shape, dt))

        s = semaphores(ctx, nc, f"l{2 * modulated}", SAMPLE_SEMS)
        t = g
        ps = g["ps"]
        img = sb("img", [128, B, QN])
        offc = sb("offc", [OT * RO, B, ROUNDS, CH])
        tok = sb("tok", [128, B, QT, 128])
        yx = sb("yx", [128, TILES * K2, 2])
        fl = sb("fl", [128, TILES * K2, 2])
        ri = sb("ri", [128, TILES * K2, 2], I32)
        gt = sb("gt", [128, TILES * K2, 2])
        fr = sb("fr", [128, TILES * K2, 2])
        qi = sb("qi", [128, TILES * K2])
        idx = sb("idx", [128, (B * TILES + SLOTS) * K2], I32)
        wts = sb("wts", [128, B * TILES * K2 * 4])
        idx_s = sb("idx_s", [128, SLOTS, K2], I32)
        wts_s = sb("wts_s", [128, SLOTS, K2 * 4])
        corner = sb("corner", [128, SLOTS, K2, 4 * 128])
        samp = sb("samp", [128, SLOTS, K2, 128])
        turned = sb("turned", [128, SLOTS, K2 * 128])
        if modulated:
            mk = sb("mk", [128, B, TILES * K2])
            wk, offw, offb = g["w_dc"], g["w_om"], g["b_om"]
        else:
            wk = sb("wk", [128, K2, 128])
            offw, offb = g["off_w"], g["off_b"]
            xg = sb("xg", [128, N])
        gap = turned[0:GUARD, 0, 0:4 * 128]
        taps = K2 if modulated else 1
        table = [nc.dram_tensor(f"table{2 * modulated}_{b}", [TROWS, 4 * 128], F32).ap() for b in range(B)]
        gather = [[s[f"gather{slot}{gr}"] for gr in range(GROUPS)] for slot in range(SLOTS)]
        filled = [s["table0"], s["table1"]]

        with nc.Block() as block:

            @block.gpsimd
            def _(pool):
                nc.gpsimd.memset(gap, 0.0).then_inc(s["gap"], 1)
                nc.gpsimd.memset(idx[:, B * TILES * K2:], 0)
                nc.gpsimd.memset(img[:, :, :], 0.0).then_inc(s["zeroed"], 1)

                def tile(b, i, slot):
                    pool.wait_ge(s["copied"], i + 1)
                    for gr in range(GROUPS):
                        pool.wait_ge(s["summed"], 3 * GROUPS * i + (3 * gr + 3))
                        pool.sem_inc(s["passed"], 1)
                        for k in range(gr * GK, (gr + 1) * GK):
                            nc.gpsimd.indirect_dma_start(
                                corner[:, slot, k, :], None, table[b],
                                bass.IndirectOffsetOnAxis(ap=idx_s[:, slot, k:k + 1], axis=0),
                            ).then_inc(gather[slot][gr], 16)

                for b in range(B):
                    pool.wait_ge(filled[b], 16 * len(CORNERS) * PARTS)
                    pool.wait_ge(s["index"], b + 1)
                    with pool.Fori(b * TILES // 2, (b + 1) * TILES // 2) as turn:
                        for slot in range(SLOTS):
                            tile(b, turn * SLOTS + slot, slot)

            @block.sync
            def _(sp):
                if not modulated:
                    load_first(sp, g)
                sp.wait_ge(s["gap"], 1)
                for b in range(B):
                    sp.dma_start(table[b][0:GUARD, :], gap).then_inc(s["gaps"], 16)
                    sp.dma_start(table[b][QN:TROWS, :], gap).then_inc(s["gaps"], 16)
                if not modulated:
                    load_rest(sp, g)
                sp.wait_ge(s["gaps"], 16 * 2 * B)
                for b, part in [(b, part) for b in range(B) for part in range(PARTS)]:
                    sp.wait_ge(s["tok"], b * QT // 4 + -(-(part + 1) * QT // (4 * PARTS)))
                    for j, d in enumerate(CORNERS):
                        lo = GUARD - d + part * QN // PARTS
                        sp.dma_start(table[b][lo:lo + QN // PARTS, j * 128:(j + 1) * 128]
                                     .rearrange("(t p) c -> p t c", p=128),
                                     tok[:, b, part * QT // PARTS:(part + 1) * QT // PARTS, :]) \
                            .then_inc(filled[b], 16)
                if not modulated:
                    stack_weights(sp, g)
                for b in range(B):
                    sp.wait_ge(filled[b], 16 * len(CORNERS) * PARTS)

            @block.scalar
            def _(act):
                act.sem_inc(s["turned"], SLOTS)

                def take_indices(i, slot):
                    nc.scalar.copy(idx_s[:, slot, :], idx[:, bass.ds(i * K2, K2)]).then_inc(s["copied"], 1)

                if not modulated:
                    act.wait_ge(g["first_loaded"], g["first_total"])
                norm_scalar(nc, act, s, t)
                if modulated:
                    nc.scalar.activation(mk[:, 0, 0:1], g["eps"][:, 0:1], ACT.Sigmoid)
                act.wait_ge(s["zeroed"], 1)
                for b in range(B):
                    if not modulated:
                        for r in range(NCH):
                            n = b * NCH + r
                            act.wait_ge(s["pw_mm"], n + 1)
                            nc.scalar.copy(window(img, b, r, 1, 1),
                                           ps[:, n % 2, 0:CH].rearrange("p (r w) -> p r w", w=W)) \
                                .then_inc(s["image"], 1)
                    for q in range(QT // 4):
                        n = b * (QT // 4) + q
                        act.wait_ge(s["tok_mm"], n + 1)
                        nc.scalar.copy(tok[:, b, 4 * q:4 * q + 4, :].rearrange("p t c -> p (t c)"),
                                       ps[:, 4 + n % 2, :]).then_inc(s["tok"], 1)
                    for rd in range(ROUNDS):
                        n = b * ROUNDS + rd
                        act.wait_ge(s["off_mm"], n + 1)
                        nc.scalar.activation(offc[:, b, rd, :], ps[0:OT * RO, 2 + n % 2, 0:CH],
                                             ACT.Identity, bias=offb[:, 0:1]).then_inc(s["offs"], 1)
                    if modulated:
                        act.wait_ge(s["ot_mm"], b + 1)
                        nc.scalar.activation(
                            mk[:, b, :].rearrange("p (a t k) -> p a t k", a=ROUNDS, k=K2),
                            ps[:, 6:8, 0:RT * RO].rearrange("p a (t r) -> p a t r", r=RO)[:, :, :, 2 * K2:3 * K2],
                            ACT.Sigmoid).then_inc(s["mask"], 1)
                    if b == 0:
                        act.wait_ge(s["index"], 1)
                        for slot in range(SLOTS):
                            take_indices(slot, slot)
                act.wait_ge(s["gaps"], 16 * 2 * B)
                act.wait_ge(s["index"], B)

                def first_corner(turn, slot, last=False):
                    i = turn * SLOTS + slot
                    act.wait_ge(s["summed"], 3 * GROUPS * i + 3 * GROUPS)
                    nc.scalar.copy(wts_s[:, slot, :], wts[:, bass.ds(i * K2 * 4, K2 * 4)]).then_inc(s["weighed"], 1)
                    act.wait_ge(s["weighed"], i + 1)
                    act.wait_ge(s["turned_mm"], i + 1)
                    for gr in range(GROUPS):
                        act.wait_ge(gather[slot][gr], turn * (16 * GK) + 16 * GK)
                        for k in range(gr * GK, (gr + 1) * GK):
                            ins = nc.scalar.activation(samp[:, slot, k, :], corner[:, slot, k, 0:128],
                                                        ACT.Copy, scale=wts_s[:, slot, 4 * k:4 * k + 1])
                        ins.then_inc(s["first_corner"], 1)
                    if not last:
                        take_indices(i + SLOTS, slot)

                def take_turned(turn, slot):
                    i = turn * SLOTS + slot
                    act.wait_ge(s["turned_mm"], i + (1 + SLOTS))
                    act.wait_ge(s["out_mm"], i + 1)
                    nc.scalar.copy(turned[:, slot, :].rearrange("p (a n) -> p a n", a=3),
                                   ps[:, 3 * slot:3 * slot + 3, 0:CH]).then_inc(s["turned"], 1)

                first_corner(0, 0)
                with act.Fori(0, TURNS - 1) as turn:
                    first_corner(turn, 1)
                    take_turned(turn, 0)
                    first_corner(turn + 1, 0)
                    take_turned(turn, 1)
                first_corner(TURNS - 1, 1, last=True)
                take_turned(TURNS - 1, 0)
                take_turned(TURNS - 1, 1)

            @block.vector
            def _(dve):
                dve.sem_inc(s["summed"], 3 * GROUPS * SLOTS)
                dve.sem_inc(s["added"], SLOTS)
                if modulated:
                    def write(b, mean, rstd):
                        dve.wait_ge(s["zeroed"], 1)
                        return nc.vector.tensor_scalar(
                            img[:, b, PW + 1:PW + 1 + H * PW].rearrange("p (r w) -> p r w", w=PW)[:, :, 0:W],
                            g["x"][:, b * S:(b + 1) * S].rearrange("p (r w) -> p r w", w=W),
                            mean, rstd, ALU.subtract, ALU.mult)
                else:
                    def write(b, mean, rstd):
                        return nc.vector.tensor_scalar(xg[:, b * S:(b + 1) * S], g["x"][:, b * S:(b + 1) * S],
                                                       mean, rstd, ALU.subtract, ALU.mult)
                norm_vector(nc, dve, s, t, write, loaded=None if modulated else g["x_loaded"])
                if not modulated:
                    dve.wait_ge(g["first_loaded"], g["first_total"])
                    for k in range(K2):
                        last = nc.vector.tensor_scalar(wk[:, k, :], g["ident"][:, :], g["dw"][:, k:k + 1], None,
                                                       ALU.mult)
                    last.then_inc(s["diag"], 1)
                chain = Chain(dve, s["chain"])
                for b in range(B):
                    dve.wait_ge(s["ot_mm"], b + 1)
                    if modulated:
                        dve.wait_ge(s["mask"], b + 1)
                    chain.link(nc.vector.tensor_tensor(
                        yx[:, :, :].rearrange("p (a t k) e -> p a t (k e)", a=ROUNDS, k=K2),
                        ps[:, 6:8, 0:RT * RO].rearrange("p a (t r) -> p a t r", r=RO)[:, :, :, 0:2 * K2],
                        g["base"][:, :].rearrange("p (a t r) -> p a t r", a=ROUNDS, r=2 * K2), ALU.add))
                    chain.link(nc.vector.tensor_scalar(yx[:, :, :], yx[:, :, :], -1.0, float(H),
                                                       ALU.max, ALU.min))
                    chain.link(nc.vector.tensor_copy(ri[:, :, :], yx[:, :, :]))
                    chain.link(nc.vector.tensor_copy(fl[:, :, :], ri[:, :, :]))
                    chain.link(nc.vector.tensor_tensor(gt[:, :, :], fl[:, :, :], yx[:, :, :], ALU.is_gt))
                    chain.link(nc.vector.tensor_tensor(fl[:, :, :], fl[:, :, :], gt[:, :, :], ALU.subtract))
                    chain.link(nc.vector.tensor_tensor(fr[:, :, :], yx[:, :, :], fl[:, :, :], ALU.subtract))
                    chain.link(nc.vector.tensor_scalar(gt[:, :, :], fr[:, :, :], -1.0, 1.0, ALU.mult, ALU.add))
                    if modulated:
                        chain.link(nc.vector.tensor_tensor(gt[:, :, 0], gt[:, :, 0], mk[:, b, :], ALU.mult))
                        chain.link(nc.vector.tensor_tensor(fr[:, :, 0], fr[:, :, 0], mk[:, b, :], ALU.mult))
                    w4 = wts[:, b * TILES * K2 * 4:(b + 1) * TILES * K2 * 4] \
                        .rearrange("p (n j) -> p n j", j=4)
                    for j, (wy, wx) in enumerate(((gt, gt), (gt, fr), (fr, gt), (fr, fr))):
                        nc.vector.tensor_tensor(w4[:, :, j], wy[:, :, 0], wx[:, :, 1], ALU.mult)
                    chain.link(nc.vector.scalar_tensor_tensor(qi[:, :], fl[:, :, 0], float(PW), fl[:, :, 1],
                                                              ALU.mult, ALU.add))
                    last = nc.vector.tensor_scalar(idx[:, b * TILES * K2:(b + 1) * TILES * K2], qi[:, :],
                                                   float(GUARD + PW + 1), None, ALU.add)
                    last.then_inc(s["index"], 1)
                    dve.wait_ge(s["index"], b + 1)
                    if not modulated and b == 0:
                        split_weights(nc, dve, g)


                def sum_corners(turn, slot):
                    i = turn * SLOTS + slot
                    for gr in range(GROUPS):
                        dve.wait_ge(s["first_corner"], GROUPS * i + (gr + 1))
                        for j in range(1, 4):
                            for k in range(gr * GK, (gr + 1) * GK):
                                last = nc.vector.scalar_tensor_tensor(
                                    samp[:, slot, k, :], corner[:, slot, k, j * 128:(j + 1) * 128],
                                    wts_s[:, slot, 4 * k + j:4 * k + j + 1], samp[:, slot, k, :],
                                    ALU.mult, ALU.add)
                            last.then_inc(s["summed"], 1)
                            if j < 3:
                                dve.wait_ge(s["summed"], 3 * GROUPS * i + (3 * GROUPS * SLOTS + 3 * gr + j))

                def add(turn, slot):
                    i = turn * SLOTS + slot
                    dve.wait_ge(s["out_mm"], i + (1 + SLOTS))
                    xt = g["x"][:, bass.ds(i * 128, 128)]
                    if modulated:
                        ins = nc.vector.scalar_tensor_tensor(xt, ps[:, 6 + slot, 0:128], g["b_dc"][:, 0:1], xt,
                                                             ALU.add, ALU.add)
                    else:
                        ins = nc.vector.tensor_tensor(xt, ps[:, 6 + slot, 0:128], xt, ALU.add)
                    ins.then_inc(s["added"], 1)
                    dve.wait_ge(s["added"], i + (1 + SLOTS))
                    nc.vector.bn_stats(g["bst"][:, :, :, :].rearrange("p b t e -> p (b t e)")[:, bass.ds(i * 6, 6)], xt)

                sum_corners(0, 0)
                with dve.Fori(0, TURNS - 1) as turn:
                    sum_corners(turn, 1)
                    add(turn, 0)
                    sum_corners(turn + 1, 0)
                    add(turn, 1)
                sum_corners(TURNS - 1, 1)
                add(TURNS - 1, 0)
                add(TURNS - 1, 1)

            @block.tensor
            def _(pe):
                if not modulated:
                    pe.wait_ge(g["first_loaded"], g["first_total"])
                norm_tensor(nc, pe, s, t)
                for b in range(B):
                    pe.wait_ge(s["norm"], b + 1)
                    if not modulated:
                        for r in range(NCH):
                            n = b * NCH + r
                            if n >= 2:
                                pe.wait_ge(s["image"], n - 1)
                            nc.tensor.matmul(ps[:, n % 2, 0:CH], g["pw"][:, :], xg[:, n * CH:(n + 1) * CH],
                                             start=True, stop=True).then_inc(s["pw_mm"], 1)
                        pe.wait_ge(s["image"], (b + 1) * NCH)
                    for q in range(QT // 4):
                        n = b * (QT // 4) + q
                        if n >= 2:
                            pe.wait_ge(s["tok"], n - 1)
                        for j in range(4):
                            at = (4 * q + j) * 128
                            last = nc.tensor.transpose(ps[:, 4 + n % 2, j * 128:(j + 1) * 128],
                                                       img[:, b, at:at + 128], g["ident"][:, :])
                        last.then_inc(s["tok_mm"], 1)
                    for rd in range(ROUNDS):
                        n = b * ROUNDS + rd
                        if n >= 2:
                            pe.wait_ge(s["offs"], n - 1)
                        for k in range(taps):
                            ky, kx = (k // 3, k % 3) if modulated else (1, 1)
                            for j in range(OT):
                                last = nc.tensor.matmul(ps[RO * j:RO * (j + 1), 2 + n % 2, 0:CH], offw[:, k, :],
                                                        window(img, b, rd * OT + j, ky, kx),
                                                        start=(k == 0), stop=(k == taps - 1),
                                                        tile_position=(0, RO * j))
                        last.then_inc(s["off_mm"], 1)
                    pe.wait_ge(s["offs"], (b + 1) * ROUNDS)
                    if b:
                        pe.wait_ge(s["index"], b)
                    for rd in range(ROUNDS):
                        into = ps[:, 6 + rd, 0:RT * RO].rearrange("p (j i r) -> p j i r", j=OT, r=RO)
                        for i in range(CH // 128):
                            last = nc.tensor.matmul(into[:, :, i, :], offc[:, b, rd, i * 128:(i + 1) * 128],
                                                    g["ident"][0:OT * RO, 0:OT * RO], start=True, stop=True)
                    last.then_inc(s["ot_mm"], 1)

                pe.wait_ge(s["tok"], B * QT // 4)
                pe.wait_ge(s["index"], B)
                if not modulated:
                    pe.wait_ge(s["diag"], 1)
                pe.sem_inc(s["turned_mm"], SLOTS)
                pe.sem_inc(s["out_mm"], SLOTS)
                with pe.Fori(0, TURNS) as turn:
                    for slot in range(SLOTS):
                        i = turn * SLOTS + slot
                        pe.wait_ge(s["summed"], 3 * GROUPS * i + 3 * GROUPS * (SLOTS + 1))
                        pe.wait_ge(s["turned"], i + 1)
                        for k in range(K2):
                            last = nc.tensor.transpose(ps[:, 3 * slot + k // 3, (k % 3) * 128:(k % 3 + 1) * 128],
                                                       samp[:, slot, k, :], g["ident"][:, :])
                        last.then_inc(s["turned_mm"], 1)
                        pe.wait_ge(s["turned"], i + 1 + SLOTS)
                        pe.wait_ge(s["added"], i + 1)
                        for k in range(K2):
                            last = nc.tensor.matmul(ps[:, 6 + slot, 0:128], wk[:, k, :],
                                                    turned[:, slot, k * 128:(k + 1) * 128],
                                                    start=(k == 0), stop=(k == K2 - 1))
                        last.then_inc(s["out_mm"], 1)


INV_SEMS = GN_SEMS + ("zeroed ones padded red_mm red rvar rstd rnorm chain relu first rest second prepared "
                      "wgt_mm products dsum psum acc_mm added")


def involution_layer(nc, g):
    with ExitStack() as ctx:
        def sb(name, shape, dt=F32):
            return ctx.enter_context(nc.sbuf_tensor(f"l1_{name}", shape, dt))

        s = semaphores(ctx, nc, "l1", INV_SEMS)
        ps = g["ps"]
        xg = sb("xg", [128, N])
        pad = sb("pad", [128, B, IN])
        red = sb("red", [RP, N])
        rst = sb("rst", [RP, B * NCH * 6])
        rmv = sb("rmv", [RP, 2])
        rsd = sb("rsd", [RP, 1])
        rrs = sb("rrs", [RP, 1])
        scale = sb("scale", [RP, 1])
        shift = sb("shift", [RP, 1])
        relu = sb("relu", [RP, 2, CH])
        first = sb("first", [RP, 2, CH], BF16)
        rest = sb("rest", [RP, 2, CH])
        mov_a = sb("mov_a", [RP + 1, N], BF16)
        mov_b = sb("mov_b", [RP + 2, N], BF16)
        prod = sb("prod", [128, 2, K7, CH])
        RING = K7
        ACC = 7
        PAIRS = B * NCH // 2
        TP, RW = 2 * TAPS, 2 * K7
        ADDS_READING = {0: 1, 1: 3, 3: 4}
        ADD_AT = 5
        FULL = (((1, 0), (3, 2), (3, 1), (6, 3)), True, (5, 6))
        LESS_POOL = (((1, 0), (3, 2), (3, 1)), True, (3, 5, 6))
        LESS_VECTOR = (((1, 0), (3, 2), (3, 1), (4, 3)), False, (4, 5, 6))
        KINDS = [FULL, FULL, FULL, LESS_VECTOR, FULL, FULL, LESS_POOL]

        def kind(row):
            return KINDS[row % K7]

        def before(row, of):
            if row < 0:
                return before(RW + row, of) - before(RW, of)
            return sum(of(kind(r)) for r in range(row))

        def pool_adds(row):
            return before(row, lambda k: len(k[0]))

        def vector_adds(row):
            return before(row, lambda k: int(k[1]))

        with nc.Block() as block:

            @block.gpsimd
            def _(pool):
                nc.gpsimd.memset(pad[:, :, :], 0.0).then_inc(s["zeroed"], 1)
                pool.wait_ge(s["zeroed"], 1)
                nc.gpsimd.memset(mov_a[RP:RP + 1, :], 1.0).then_inc(s["ones"], 1)
                pool.wait_ge(s["ones"], 1)
                nc.gpsimd.memset(mov_b[RP:RP + 2, :], 1.0).then_inc(s["ones"], 1)
                pool.wait_ge(s["ones"], 2)
                for b in range(B):
                    pool.wait_ge(s["norm"], b + 1)
                    nc.gpsimd.tensor_copy(
                        pad[:, b, 3 * IW:3 * IW + H * IW].rearrange("p (r w) -> p r w", w=IW)[:, :, 3:3 + W],
                        xg[:, b * S:(b + 1) * S].rearrange("p (r w) -> p r w", w=W)).then_inc(s["padded"], 1)
                with pool.Fori(0, PAIRS) as pair:
                    for row in range(RW):
                        q = row % 2

                        def add(i, j):
                            nc.gpsimd.tensor_tensor(prod[:, q, i, :], prod[:, q, i, :], prod[:, q, j, :],
                                                    ALU.add).then_inc(s["psum"], 1)

                        done = pair * TP + (row * K7 + RING)
                        sums = pair * pool_adds(RW)
                        for n, (i, j) in enumerate(kind(row)[0]):
                            if n < 2:
                                pool.wait_ge(s["products"], done + 2 * n + 2)
                            else:
                                pool.wait_ge(s["psum"], sums + (pool_adds(row) + n))
                            if i >= 4:
                                pool.wait_ge(s["products"], done + i + 1)
                            add(i, j)

            @block.scalar
            def _(act):
                norm_scalar(nc, act, s, g)
                for n in range(B * NCH):
                    act.wait_ge(s["red_mm"], n + 1)
                    nc.scalar.activation(red[:, n * CH:(n + 1) * CH], ps[0:RP, n % 2, 0:CH], ACT.Identity,
                                         bias=g["b1"][:, 0:1]).then_inc(s["red"], 1)
                act.wait_ge(s["rvar"], 1)
                nc.scalar.activation(rsd[:, :], rmv[:, 1:2], ACT.Sqrt, bias=g["eps"][0:RP, 0:1]).then_inc(s["rstd"], 1)
                act.wait_ge(s["rnorm"], 1)

                def prepare(c, h):
                    at = bass.ds(c * CH, CH)
                    act.wait_ge(s["rest"], c + 1)
                    nc.scalar.activation(relu[:, h, :], red[:, at], ACT.Relu, bias=shift[:, 0:1],
                                         scale=scale[:, 0:1])
                    nc.scalar.activation(first[:, h, :], red[:, at], ACT.Relu, bias=shift[:, 0:1],
                                         scale=scale[:, 0:1]).then_inc(s["first"], 1)
                    act.wait_ge(s["first"], c + 1)
                    nc.scalar.copy(mov_a[0:2 * RED, at], first[0:2 * RED, h, :])
                    nc.scalar.copy(mov_b[0:RED, at], first[0:RED, h, :])
                    act.wait_ge(s["rest"], c + (1 + 2))
                    nc.scalar.copy(mov_b[RED:2 * RED, at], rest[RED:2 * RED, h, :])
                    nc.scalar.copy(mov_a[2 * RED:RP, at], rest[2 * RED:RP, h, :]).then_inc(s["second"], 1)

                for c in range(2):
                    prepare(c, c)
                with act.Fori(0, PAIRS - 1) as pair:
                    for h in range(2):
                        prepare(pair * 2 + (2 + h), h)

            @block.vector
            def _(dve):
                def write(b, mean, rstd):
                    return nc.vector.tensor_scalar(xg[:, b * S:(b + 1) * S], g["x"][:, b * S:(b + 1) * S],
                                                   mean, rstd, ALU.subtract, ALU.mult)
                norm_vector(nc, dve, s, g, write, stats=TILES)
                chain = Chain(dve, s["chain"])
                for n in range(B * NCH):
                    dve.wait_ge(s["red"], n + 1)
                    last = nc.vector.bn_stats(rst[:, n * 6:(n + 1) * 6], red[:, n * CH:(n + 1) * CH])
                chain.link(last)
                nc.vector.bn_aggr(rmv[:, :], rst[:, :]).then_inc(s["rvar"], 1)
                dve.wait_ge(s["rstd"], 1)
                chain.link(nc.vector.reciprocal(rrs[:, :], rsd[:, :]))
                chain.link(nc.vector.tensor_tensor(scale[:, :], rrs[:, :], g["gamma"][:, :], ALU.mult))
                chain.link(nc.vector.tensor_tensor(shift[:, :], rmv[:, 0:1], scale[:, :], ALU.mult))
                nc.vector.tensor_tensor(shift[:, :], g["beta"][:, :], shift[:, :], ALU.subtract).then_inc(s["rnorm"], 1)
                dve.sem_inc(s["rest"], 2)

                def take_rest(c, h):
                    dve.wait_ge(s["first"], c + 1)
                    nc.vector.tensor_tensor(rest[:, h, :], relu[:, h, :], first[:, h, :],
                                            ALU.subtract).then_inc(s["rest"], 1)

                def third_part(c, h):
                    dve.wait_ge(s["second"], c + 1)
                    at = bass.ds(c * CH, CH)
                    nc.vector.tensor_tensor(mov_b[2 * RED:RP, at], rest[2 * RED:RP, h, :],
                                            mov_a[2 * RED:RP, at], ALU.subtract).then_inc(s["prepared"], 1)

                for c in range(2):
                    take_rest(c, c)
                    third_part(c, c)
                dve.wait_ge(s["padded"], 1)
                dve.sem_inc(s["products"], RING)
                dve.sem_inc(s["added"], 1)
                flat = pad[:, :, :].rearrange("p b n -> p (b n)")

                def into_x(c):
                    xt = g["x"][:, bass.ds(c * CH, CH)]
                    nc.vector.tensor_tensor(xt, ps[:, ACC, 0:CH], xt, ALU.add).then_inc(s["added"], 1)

                STEPS = {2: (take_rest, 0), 5: (third_part, 0), 8: (take_rest, 1), 11: (third_part, 1)}

                def rows(pair, b, r2, first=False, last=False):
                    for row in range(RW):
                        half, ky = divmod(row, K7)
                        if row in STEPS and not last:
                            step, h = STEPS[row]
                            step(pair * 2 + (2 + h), h)
                        for kx in range(K7):
                            if kx == kind(row - 2)[2][0]:
                                dve.wait_ge(s["acc_mm"], pair * RW + (row + 1))
                            elif kx in ADDS_READING and not (first and row < 2):
                                dve.wait_ge(s["psum"], pair * pool_adds(RW) + (pool_adds(row - 2) + ADDS_READING[kx]))
                            dve.wait_ge(s["wgt_mm"], pair * TP + (row * K7 + kx + 1))
                            src = flat[:, bass.ds(b * IN + r2 * (2 * ROWS * IW) + (half * ROWS + ky) * IW,
                                                  ROWS * IW)] \
                                .rearrange("p (r w) -> p r w", w=IW)[:, :, kx:kx + W]
                            nc.vector.tensor_tensor(
                                prod[:, row % 2, kx, :].rearrange("p (r w) -> p r w", w=W),
                                ps[:, kx, 0:CH].rearrange("p (r w) -> p r w", w=W), src, ALU.mult) \
                                .then_inc(s["products"], 1)
                        if kind(row)[1]:
                            dve.wait_ge(s["products"], pair * TP + (row * K7 + K7 - 1 + RING))
                            nc.vector.tensor_tensor(prod[:, row % 2, 5, :], prod[:, row % 2, 5, :],
                                                    prod[:, row % 2, 4, :], ALU.add).then_inc(s["dsum"], 1)
                        if row == 1 and not first:
                            dve.wait_ge(s["acc_mm"], pair * RW + 2)
                            into_x(pair * 2 - 1)
                        if row == K7 + 1:
                            dve.wait_ge(s["acc_mm"], pair * RW + (K7 + 2))
                            into_x(pair * 2)

                rows(0, 0, 0, first=True)
                with dve.Fori(1, NCH // 2) as r2:
                    rows(r2, 0, r2)
                dve.wait_ge(s["padded"], B)
                with dve.Fori(0, NCH // 2 - 1) as r2:
                    rows(r2 + NCH // 2, 1, r2)
                rows(PAIRS - 1, 1, NCH // 2 - 1, last=True)
                dve.wait_ge(s["acc_mm"], PAIRS * RW + 2)
                into_x(B * NCH - 1)

            @block.tensor
            def _(pe):
                norm_tensor(nc, pe, s, g)
                for n in range(B * NCH):
                    pe.wait_ge(s["norm"], n // NCH + 1)
                    if n >= 2:
                        pe.wait_ge(s["red"], n - 1)
                    nc.tensor.matmul(ps[0:RP, n % 2, 0:CH], g["w1"][:, :], xg[:, n * CH:(n + 1) * CH],
                                     start=True, stop=True).then_inc(s["red_mm"], 1)
                pe.wait_ge(s["red"], B * NCH)
                pe.wait_ge(s["ones"], 2)
                pe.sem_inc(s["acc_mm"], 2)

                def weights(pair, row, kx):
                    tap, k = row * K7 + kx, row * K7 % TAPS + kx
                    at = bass.ds(pair * (2 * CH) + (row // K7) * CH, CH)
                    pe.wait_ge(s["products"], pair * TP + (tap + 1))
                    nc.tensor.matmul(ps[:, kx, 0:CH], g["wgt_a"][:, k * 128:(k + 1) * 128], mov_a[:, at],
                                     start=True, stop=False)
                    nc.tensor.matmul(ps[:, kx, 0:CH], g["wgt_b"][:, k * 128:(k + 1) * 128], mov_b[:, at],
                                     start=False, stop=True).then_inc(s["wgt_mm"], 1)

                def add(pair, row):
                    pe.wait_ge(s["psum"], pair * pool_adds(RW) + pool_adds(row + 1))
                    pe.wait_ge(s["dsum"], pair * vector_adds(RW) + vector_adds(row + 1))
                    pe.wait_ge(s["products"], pair * TP + ((row + 1) * K7 + RING))
                    if row % K7 == 0:
                        pe.wait_ge(s["added"], pair * 2 + (row // K7 + 1))
                    for j in kind(row)[2]:
                        last = nc.tensor.matmul(ps[:, ACC, 0:CH], g["ident"][:, :], prod[:, row % 2, j, :],
                                                start=(row % K7 == 0 and j == kind(row)[2][0]),
                                                stop=(row % K7 == K7 - 1 and j == kind(row)[2][-1]))
                    last.then_inc(s["acc_mm"], 1)

                def rows(pair, first):
                    pe.wait_ge(s["prepared"], pair * 2 + 2)
                    for row in range(RW):
                        for kx in range(K7):
                            weights(pair, row, kx)
                            if kx == ADD_AT and not (first and row < 2):
                                add(pair, row - 2)

                rows(0, True)
                with pe.Fori(1, PAIRS) as pair:
                    rows(pair, False)
                add(PAIRS, -2)
                add(PAIRS, -1)


ATT_SEMS = GN_SEMS + ("const proj part1 part2 split v_mm v_all stored kmax0 kmax1 key0 key1 query0 query1 query2 "
                      "v_slot st_mm exp av_mm a_mm max negmax nsplit rows_mm rows o_sb ot_mm ochain out z_in "
                      "zt_mm zt z_mm z_added saved pchain passed")


def attention_layer(nc, g, out):
    with ExitStack() as ctx:
        def sb(name, shape, dt=F32):
            return ctx.enter_context(nc.sbuf_tensor(f"l3_{name}", shape, dt))

        s = semaphores(ctx, nc, "l3", ATT_SEMS)
        ps = g["ps"]
        xg = sb("xg", [128, N])
        part = sb("part", [128, B, 2, 3, S], BF16)
        rest = sb("rest", [128, 2, CH])
        v_all = sb("v_all", [128, NH, KT, HD])
        v_s = sb("v_s", [128, 2, KT, 32])
        qs = sb("qs", [KROWS + MROWS, 3, CT * QC], BF16)
        ks = sb("ks", [KROWS + MROWS, 2, S], BF16)
        ka = sb("ka", [KROWS, 2, S], BF16)
        e = sb("e", [128, ERING, CT, QC])
        mx = sb("mx", [128, 2, 3, NQC])
        nm = sb("nm", [128, 2, 3])
        nr = sb("nr", [128, 2, 3])
        nsp = sb("nsp", [128, 2, 3, MROWS], BF16)
        identb = sb("identb", [128, 128], BF16)
        o_s = sb("o_s", [128, QC])
        rec = sb("rec", [128, 3, CT])
        o_t = sb("o_t", [128, CT + CHUNKS, 3, HD])
        z_in = sb("z_in", [128, 2, 3, C])
        z_t = sb("z_t", [128, 2, CH])
        stack = nc.dram_tensor("qk_parts", [2 * 3 * B * 128, S], BF16).ap()
        ST, AB, AV, MISC = 0, 3, 6, 7
        RING = 3
        kmax = [s["kmax0"], s["kmax1"]]
        key = [s["key0"], s["key1"]]
        query = [s["query0"], s["query1"], s["query2"]]
        KEY_LOADS = 16 * len(K_PARTS)
        PIECES = [[(0, 0, 0, CT * QC)],
                  [(0, CT * QC, 0, S - CT * QC), (1, 0, S - CT * QC, 2 * CT * QC - S)],
                  [(1, 2 * CT * QC - S, 0, CT * QC)]]
        BATCHES = len(PIECES)
        PAIRS = NH // 2
        UNITS = CT * KT
        V_TILES = N // 128
        ROWS_AT = (1, 6, 10, 15)
        TURN_AT = 3
        Z_AT = {5 + 2 * c: c for c in range(NCH)}

        def z_banks(c):
            return (AB if c < NCH else ST + c % 2), AB + 1 + c % 2

        def gather_heads(engine, c):
            b, r = divmod(c, NCH)
            g0 = CT + b * HEADS * NQC + r
            return engine.tensor_copy(
                z_in[:, c % 2, :, :].rearrange("p i (h d) -> p i h d", d=HD),
                o_t[:, g0:g0 + (HEADS - 1) * NQC + 1:NQC, :, :].rearrange("p h i d -> p i h d"))


        with nc.Block() as block:

            @block.sync
            def _(sp):
                def store(b):
                    for side in range(2):
                        sp.wait_ge(s["split"], (2 * b + side + 1) * NCH)
                        for p in range(3):
                            r0 = (side * 3 + p) * B * 128 + b * 128
                            sp.dma_start(stack[r0:r0 + 128, :], part[:, b, side, p, :]).then_inc(s["stored"], 16)
                    sp.wait_ge(s["stored"], 16 * 3 * 2 * (b + 1))

                def keys(n, tile, slot, sem):
                    for i, p in enumerate(K_PARTS):
                        sp.dma_start(tile[HD * i:HD * (i + 1), slot, :],
                                     stack[bass.ds(n * HD + (3 + p) * B * 128, HD), :]).then_inc(sem[slot], 16)

                def queries(m, k):
                    for head, q0, at, n in PIECES[k]:
                        for i, p in enumerate(Q_PARTS):
                            sp.dma_start(qs[HD * i:HD * (i + 1), k, at:at + n],
                                         stack[bass.ds(m * (2 * HD) + (head * HD + p * B * 128), HD), q0:q0 + n]) \
                                .then_inc(query[k], 16)

                store(0)
                queries(0, 0)
                keys(0, ka, 0, kmax)
                queries(0, 1)
                keys(0, ks, 0, key)
                keys(1, ka, 1, kmax)
                keys(1, ks, 1, key)
                queries(0, 2)
                store(1)
                with sp.Fori(0, PAIRS - 1) as m:
                    sp.wait_ge(s["a_mm"], m * (2 * NQC * KT) + NQC * KT)
                    keys(m * 2 + 2, ka, 0, kmax)
                    sp.wait_ge(s["st_mm"], m * (BATCHES * UNITS) + UNITS)
                    queries(m + 1, 0)
                    sp.wait_ge(s["a_mm"], m * (2 * NQC * KT) + 2 * NQC * KT)
                    keys(m * 2 + 3, ka, 1, kmax)
                    sp.wait_ge(s["st_mm"], m * (BATCHES * UNITS) + 2 * UNITS)
                    keys(m * 2 + 2, ks, 0, key)
                    queries(m + 1, 1)
                    sp.wait_ge(s["st_mm"], m * (BATCHES * UNITS) + 3 * UNITS)
                    queries(m + 1, 2)
                    keys(m * 2 + 3, ks, 1, key)
                for c in range(B * NCH):
                    sp.wait_ge(s["z_added"], c + 1)
                    b, r = divmod(c, NCH)
                    sp.dma_start(out[b, :, r * CH:(r + 1) * CH], g["x"][:, c * CH:(c + 1) * CH]).then_inc(s["saved"], 16)
                sp.wait_ge(s["saved"], 16 * B * NCH)

            @block.gpsimd
            def _(pool):
                chain = Chain(pool, s["pchain"])
                chain.link(nc.gpsimd.memset(v_s[:, :, :, HD:32], 0.0))
                chain.link(nc.gpsimd.memset(ks[KROWS:KROWS + MROWS, :, :], 1.0))
                chain.link(nc.gpsimd.memset(o_s[:, :], 1.0))
                chain.link(nc.gpsimd.tensor_copy(identb[:, :], g["ident"][:, :]))
                nc.gpsimd.memset(v_s[:, :, :, HD:HD + 1], 1.0).then_inc(s["const"], 1)
                for b in range(B):
                    for side in range(2):
                        for r in range(NCH):
                            n = (2 * b + side) * NCH + r
                            pool.wait_ge(s["part2"], 2 * n + 2)
                            nc.gpsimd.tensor_tensor(part[:, b, side, 2, r * CH:(r + 1) * CH], rest[:, n % 2, :],
                                                    part[:, b, side, 1, r * CH:(r + 1) * CH], ALU.subtract) \
                                .then_inc(s["split"], 1)

                def take_v(n, slot):
                    nc.gpsimd.tensor_copy(
                        v_s[:, slot, :, 0:HD],
                        v_all[:, :, :, :].rearrange("p n t d -> p (n t d)")[:, bass.ds(n * (KT * HD), KT * HD)]
                        .rearrange("p (t d) -> p t d", d=HD)).then_inc(s["v_slot"], 1)

                def split_max(ga, slot):
                    pool.wait_ge(s["negmax"], ga + 1)
                    pool.sem_inc(s["passed"], 1)
                    n1, n2, n3 = (nsp[:, slot, :, i] for i in range(3))
                    chain.link(nc.gpsimd.tensor_copy(n1, nm[:, slot, :]))
                    chain.link(nc.gpsimd.tensor_tensor(nr[:, slot, :], nm[:, slot, :], n1, ALU.subtract))
                    pool.sem_inc(s["passed"], 1)
                    chain.link(nc.gpsimd.tensor_copy(n2, nr[:, slot, :]))
                    nc.gpsimd.tensor_tensor(n3, nr[:, slot, :], n2, ALU.subtract).then_inc(s["nsplit"], 1)

                for ga in range(AHEAD):
                    if ga >= 2:
                        pool.wait_ge(s["rows_mm"], ga - 1)
                    split_max(ga, ga % 2)
                pool.wait_ge(s["v_all"], V_TILES)
                pool.wait_ge(s["const"], 1)
                pool.sem_inc(s["passed"], 1)
                take_v(0, 0)

                def pair(m, last):
                    for k in range(BATCHES):
                        if k == 0 or (k == 2 and not last):
                            pool.wait_ge(s["av_mm"], m * (BATCHES * KT) + (k * KT + ERING))
                            pool.sem_inc(s["passed"], 1)
                            take_v(m * 2 + 1 + k // 2, 1 - k // 2)
                        for i in range(CT):
                            ahead = k * CT + i + AHEAD
                            if not (last and ahead >= 2 * NQC):
                                pool.wait_ge(s["rows_mm"], m * (2 * NQC) + (ahead - 1))
                                split_max(m * (2 * NQC) + ahead, ahead % 2)

                start = chain.count
                with pool.Fori(0, PAIRS - 1) as m:
                    chain.base = m * (3 * 2 * NQC)
                    pair(m, False)
                links = chain.count - start
                assert links == 3 * 2 * NQC
                chain.base, chain.count = 0, start + links * (PAIRS - 1)
                pair(PAIRS - 1, True)
                pool.wait_ge(s["out"], PAIRS * BATCHES // B + 2)
                for c in range(NCH):
                    if c >= 2:
                        pool.wait_ge(s["zt_mm"], c - 1)
                    gather_heads(nc.gpsimd, c).then_inc(s["z_in"], 1)

            @block.scalar
            def _(act):
                norm_scalar(nc, act, s, g)
                for b in range(B):
                    for side in range(2):
                        for r in range(NCH):
                            n = (2 * b + side) * NCH + r
                            act.wait_ge(s["proj"], n + 1)
                            nc.scalar.activation(part[:, b, side, 0, r * CH:(r + 1) * CH], ps[:, n % 2, 0:CH],
                                                 ACT.Copy, scale=HD ** -0.5 if side == 0 else 1.0) \
                                .then_inc(s["part1"], 1)

                def take_values(n):
                    b, t = divmod(n, TILES)
                    act.wait_ge(s["v_mm"], n + 1)
                    nc.scalar.copy(v_all[:, b * HEADS:(b + 1) * HEADS, t, :],
                                   ps[:, ST + n % 2, 0:128].rearrange("p (h d) -> p h d", d=HD)) \
                        .then_inc(s["v_all"], 1)

                act.wait_ge(s["const"], 1)
                act.sem_inc(s["exp"], RING)

                def exp(step, kt, i):
                    slot = kt % ERING
                    act.wait_ge(s["st_mm"], step * CT + (i + 1))
                    act.wait_ge(s["av_mm"], step + 1)
                    nc.scalar.activation(e[:, slot, i, :], ps[:, ST + (kt * CT + i) % RING, 0:QC], ACT.Exp).then_inc(s["exp"], 1)

                def rows(gr, slot, i):
                    act.wait_ge(s["rows_mm"], gr + 1)
                    nc.scalar.copy(qs[KROWS:KROWS + MROWS, slot, i * QC:(i + 1) * QC],
                                   ps[KROWS:KROWS + MROWS, MISC, 0:QC]).then_inc(s["rows"], 1)

                for ga in range(AHEAD):
                    for n in range(ga * KT // 2, min((ga + 1) * KT // 2, V_TILES)):
                        take_values(n)
                    if ga:
                        rows(ga - 1, 0, ga - 1)
                for i in range(CT):
                    exp(0, 0, i)

                def pair(m, last):
                    for k in range(BATCHES):
                        gb = m * BATCHES + k
                        end = last and k == BATCHES - 1
                        for kt in range(KT):
                            if not (end and kt == KT - 1):
                                for i in range(CT):
                                    exp(gb * KT + (kt + 1), kt + 1, i)
                            if kt in ROWS_AT and not end:
                                i = ROWS_AT.index(kt)
                                rows(gb * CT + (CT + i), (k + 1) % BATCHES, i)
                        act.wait_ge(s["av_mm"], gb * KT + (KT + ERING))
                        act.wait_ge(s["ot_mm"], gb + 1)
                        nc.scalar.copy(o_s[:, :], ps[:, AV, 0:QC]).then_inc(s["o_sb"], 1)

                with act.Fori(0, PAIRS - 1) as m:
                    pair(m, False)
                pair(PAIRS - 1, True)
                for c in range(NCH, B * NCH):
                    act.wait_ge(s["zt_mm"], c + 1)
                    act.wait_ge(s["z_mm"], c - 1)
                    nc.scalar.copy(z_t[:, c % 2, :], ps[:, z_banks(c)[0], 0:CH]).then_inc(s["zt"], 1)

            @block.vector
            def _(dve):
                def write(b, mean, rstd):
                    return nc.vector.tensor_scalar(xg[:, b * S:(b + 1) * S], g["x"][:, b * S:(b + 1) * S],
                                                   mean, rstd, ALU.subtract, ALU.mult)
                norm_vector(nc, dve, s, g, write, stats=TILES)
                for b in range(B):
                    for side in range(2):
                        for r in range(NCH):
                            n = (2 * b + side) * NCH + r
                            p0, p1 = (part[:, b, side, i, r * CH:(r + 1) * CH] for i in range(2))
                            dve.wait_ge(s["part1"], n + 1)
                            if n >= 2:
                                dve.wait_ge(s["split"], n - 1)
                            nc.vector.scalar_tensor_tensor(rest[:, n % 2, :], ps[:, n % 2, 0:CH],
                                                           HD ** -0.5 if side == 0 else 1.0, p0,
                                                           ALU.mult, ALU.subtract).then_inc(s["part2"], 1)
                            dve.wait_ge(s["part2"], 2 * n + 1)
                            nc.vector.tensor_copy(p1, rest[:, n % 2, :]).then_inc(s["part2"], 1)
                dve.sem_inc(s["max"], RING)

                def reduce(ga, slot, u):
                    dve.wait_ge(s["a_mm"], ga * KT + (u + 1))
                    nc.vector.tensor_reduce(mx[:, slot, u // NQC, u % NQC:u % NQC + 1],
                                            ps[:, AB + u % RING, 0:CH], AX.X, ALU.max).then_inc(s["max"], 1)
                    if u == KT - 1:
                        dve.wait_ge(s["max"], ga * KT + (KT + RING))
                        nc.vector.tensor_reduce(nm[:, slot, :], mx[:, slot, :, :], AX.X, ALU.max, negate=True) \
                            .then_inc(s["negmax"], 1)

                for ga in range(AHEAD):
                    if ga >= 2:
                        dve.wait_ge(s["nsplit"], ga - 1)
                    for u in range(KT):
                        reduce(ga, ga % 2, u)

                def normalise(at):
                    dve.wait_ge(s["ot_mm"], at + 1)
                    sums = ps[:, MISC, 0:3 * 128].rearrange("p (t i d) -> p t i d", t=3, d=32)
                    nc.vector.reciprocal(rec[:, :, :], sums[:, :, :, HD]).then_inc(s["ochain"], 1)
                    dve.wait_ge(s["ochain"], at + 1)
                    size = CT * 3 * HD
                    nc.vector.tensor_tensor(
                        o_t[:, :, :, :].rearrange("p g t d -> p (g t d)")[:, bass.ds(at * size, size)]
                        .rearrange("p (i t d) -> p t i d", t=3, d=HD),
                        sums[:, :, :, 0:HD], rec[:, :, :].unsqueeze(3).to_broadcast([128, 3, CT, HD]), ALU.mult) \
                        .then_inc(s["out"], 1)

                def pair(m, last):
                    for k in range(BATCHES):
                        for kt in range(KT):
                            for i in range(CT):
                                ahead, u = divmod(k * UNITS + kt * CT + i, KT)
                                ahead += AHEAD
                                if not (last and ahead >= 2 * NQC):
                                    if u == 2:
                                        dve.wait_ge(s["nsplit"], m * (2 * NQC) + (ahead - 1))
                                    reduce(m * (2 * NQC) + ahead, ahead % 2, u)
                                if kt == TURN_AT + 1 and i == 0:
                                    normalise(m * BATCHES + k)
                            if last and k == BATCHES - 1:
                                if kt in Z_AT:
                                    c = Z_AT[kt]
                                    dve.wait_ge(s["zt_mm"], c + 1)
                                    nc.vector.tensor_copy(z_t[:, c % 2, :], ps[:, z_banks(c)[0], 0:CH]) \
                                        .then_inc(s["zt"], 1)
                                if kt - 1 in Z_AT:
                                    add_z(Z_AT[kt - 1])

                def add_z(c):
                    dve.wait_ge(s["z_mm"], c + 1)
                    xt = g["x"][:, c * CH:(c + 1) * CH]
                    nc.vector.tensor_tensor(xt, ps[:, z_banks(c)[1], 0:CH], xt, ALU.add).then_inc(s["z_added"], 1)

                with dve.Fori(0, PAIRS - 1) as m:
                    pair(m, False)
                pair(PAIRS - 1, True)
                normalise(PAIRS * BATCHES)
                dve.wait_ge(s["out"], PAIRS * BATCHES + 2)
                for c in range(NCH, B * NCH + 2):
                    if c < B * NCH:
                        dve.wait_ge(s["zt_mm"], c - 1)
                        gather_heads(nc.vector, c).then_inc(s["z_in"], 1)
                    if c >= NCH + 2:
                        add_z(c - 2)

            @block.tensor
            def _(pe):
                norm_tensor(nc, pe, s, g)
                for b in range(B):
                    pe.wait_ge(s["norm"], b + 1)
                    for side in range(2):
                        for r in range(NCH):
                            n = (2 * b + side) * NCH + r
                            if n >= 2:
                                pe.wait_ge(s["part2"], 2 * n - 3)
                            nc.tensor.matmul(ps[:, n % 2, 0:CH], g["wqk"][:, side, :],
                                             xg[:, b * S + r * CH:b * S + (r + 1) * CH],
                                             start=True, stop=True).then_inc(s["proj"], 1)
                pe.wait_ge(s["part2"], 2 * 2 * B * NCH)
                pe.wait_ge(s["const"], 1)
                pe.sem_inc(s["av_mm"], ERING)

                def scores(m, step, chunk, kt):
                    i = chunk % CT
                    if chunk % NQC == 0 and kt == 0:
                        pe.wait_ge(key[chunk // NQC % 2], m * KEY_LOADS + (chunk // NQC // 2 + 1) * KEY_LOADS)
                    pe.wait_ge(s["exp"], step * CT + (i + 1))
                    nc.tensor.matmul(ps[:, ST + (kt * CT + i) % RING, 0:QC], ks[:, chunk // NQC % 2, kt * 128:(kt + 1) * 128],
                                     qs[:, chunk // CT % BATCHES, i * QC:(i + 1) * QC], start=True, stop=True) \
                        .then_inc(s["st_mm"], 1)

                def by_query(m, chunk, u):
                    if chunk % CT == 0 and u == 0:
                        turn, slot = divmod(chunk // CT, BATCHES)
                        loads = 16 * len(Q_PARTS) * len(PIECES[slot])
                        pe.wait_ge(query[slot], m * loads + (turn + 1) * loads)
                    if chunk % NQC == 0 and u == 0:
                        pe.wait_ge(kmax[chunk // NQC % 2], m * KEY_LOADS + (chunk // NQC // 2 + 1) * KEY_LOADS)
                    pe.wait_ge(s["max"], m * (2 * NQC * KT) + (chunk * KT + u + 1))
                    q0 = chunk % CT * QC + (u // NQC) * 128
                    nc.tensor.matmul(ps[:, AB + u % RING, 0:CH], qs[0:KROWS, chunk // CT % BATCHES, q0:q0 + 128],
                                     ka[:, chunk // NQC % 2, (u % NQC) * CH:(u % NQC + 1) * CH],
                                     start=True, stop=True).then_inc(s["a_mm"], 1)

                def rows(gr, slot):
                    pe.wait_ge(s["nsplit"], gr + 1)
                    for i in range(3):
                        last = nc.tensor.matmul(ps[KROWS:KROWS + MROWS, MISC, i * 128:(i + 1) * 128],
                                                nsp[:, slot, i, :], identb[:, :], start=True, stop=True,
                                                tile_position=(0, KROWS))
                    last.then_inc(s["rows_mm"], 1)

                def turn_sums(gb):
                    for i in range(3):
                        last = nc.tensor.transpose(ps[:, MISC, i * 128:(i + 1) * 128], o_s[:, i * 128:(i + 1) * 128],
                                                   g["ident"][:, :])
                    last.then_inc(s["ot_mm"], 1)

                def values(n):
                    if n >= 2:
                        pe.wait_ge(s["v_all"], n - 1)
                    nc.tensor.matmul(ps[:, ST + n % 2, 0:128], xg[:, n * 128:(n + 1) * 128], g["wv"][:, :],
                                     start=True, stop=True).then_inc(s["v_mm"], 1)

                for ga in range(AHEAD):
                    for u in range(KT):
                        by_query(0, ga, u)
                        if u % 2 and ga * KT + u < 2 * V_TILES:
                            values((ga * KT + u) // 2)
                    if ga:
                        if ga >= 2:
                            pe.wait_ge(s["rows"], ga - 1)
                        rows(ga - 1, (ga - 1) % 2)
                pe.wait_ge(s["rows"], CT)
                pe.wait_ge(s["v_all"], V_TILES)
                for i in range(CT):
                    scores(0, 0, i, 0)

                def pair(m, last):
                    for k in range(BATCHES):
                        gb = m * BATCHES + k
                        end = last and k == BATCHES - 1
                        if k < 2:
                            pe.wait_ge(s["v_slot"], m * 2 + (k + 1))
                        for kt in range(KT):
                            if kt == KT - 1 and not end:
                                pe.wait_ge(s["rows"], gb * CT + 2 * CT)
                            for i in range(CT):
                                ahead, u = divmod(k * UNITS + kt * CT + i, KT)
                                if not (last and ahead + AHEAD >= 2 * NQC):
                                    by_query(m, ahead + AHEAD, u)
                                if kt + 1 < KT:
                                    scores(m, gb * KT + (kt + 1), k * CT + i, kt + 1)
                                elif not end:
                                    scores(m, gb * KT + KT, (k + 1) * CT + i, 0)
                            pe.wait_ge(s["exp"], gb * UNITS + (CT * (kt + 1) + RING))
                            if kt == 0:
                                pe.wait_ge(s["o_sb"], gb + 1)
                            for i in range(CT):
                                last_mm = nc.tensor.matmul(
                                    ps[32 * i:32 * i + 32, AV, 0:QC], v_s[:, (k * CT + i) // NQC, kt, :],
                                    e[:, kt % ERING, i, :],
                                    start=(kt == 0), stop=(kt == KT - 1), tile_position=(0, 32 * i))
                            last_mm.then_inc(s["av_mm"], 1)
                            if kt in ROWS_AT and not end:
                                i = ROWS_AT.index(kt)
                                pe.wait_ge(s["rows"], gb * CT + (CT + i))
                                pe.wait_ge(s["out"], gb + (kt > TURN_AT) + 1)
                                rows(gb * CT + (CT + i), (CT + i) % 2)
                            if kt == TURN_AT:
                                if not end:
                                    pe.wait_ge(s["rows"], gb * CT + (CT + 1))
                                turn_sums(gb)
                            if end:
                                if kt - 1 in Z_AT:
                                    project(Z_AT[kt - 1])
                                if kt in Z_AT:
                                    turn_heads(Z_AT[kt])

                def turn_heads(c):
                    pe.wait_ge(s["z_in"], c + 1)
                    if c == 0:
                        pe.wait_ge(s["max"], CHUNKS * KT + RING)
                    elif c <= NCH:
                        pe.wait_ge(s["zt"], c)
                    else:
                        pe.wait_ge(s["zt"], c - 1)
                    for i in range(3):
                        last = nc.tensor.transpose(ps[:, z_banks(c)[0], i * 128:(i + 1) * 128], z_in[:, c % 2, i, :],
                                                   g["ident"][:, :])
                    last.then_inc(s["zt_mm"], 1)

                def project(c):
                    pe.wait_ge(s["zt"], c + 1)
                    if c >= 2:
                        pe.wait_ge(s["z_added"], c - 1)
                    nc.tensor.matmul(ps[:, z_banks(c)[1], 0:CH], g["wo"][:, :], z_t[:, c % 2, :],
                                     start=True, stop=True).then_inc(s["z_mm"], 1)

                pe.sem_inc(s["o_sb"], 1)
                pe.sem_inc(s["out"], 1)
                with pe.Fori(0, PAIRS - 1) as m:
                    pair(m, False)
                pair(PAIRS - 1, True)
                pe.wait_ge(s["o_sb"], PAIRS * BATCHES + 1)
                pe.wait_ge(s["out"], PAIRS * BATCHES + 1)
                turn_sums(PAIRS * BATCHES)
                turn_heads(NCH)
                for c in range(NCH, B * NCH):
                    if c + 1 < B * NCH:
                        turn_heads(c + 1)
                    project(c)


CONSTS = [
    ("ident", [128, 128]), ("gavg", [128, 128]), ("base", [128, TILES * 2 * K2]),
    ("pw", [128, 128]), ("off_w", [128, 1, RO]), ("off_b", [OT * RO, 1]), ("dw", [128, K2]),
    ("w1", [128, RP]), ("b1", [RP, 1]), ("gamma", [RP, 1]), ("beta", [RP, 1]),
    ("w2", [WQ * RED, TAPS * C // WQ]), ("b2", [TAPS, C]),
    ("w_om", [128, K2, RO]), ("b_om", [OT * RO, 1]), ("w_dc", [128, K2, 128]), ("b_dc", [128, 1]),
    ("wqk", [128, 2, 128]), ("wv", [128, 128]), ("wo", [128, 128]),
]


FIRST = 7


def load_first(sp, g):
    for b in range(B):
        sp.dma_start(g["x"][:, b * S:(b + 1) * S], g["in_x"][b, :, :]).then_inc(g["x_loaded"][b], 16)
    for name, shape in CONSTS[:FIRST]:
        sp.dma_start(g[name][:], g["consts"][name]).then_inc(g["first_loaded"], 16)


def load_rest(sp, g):
    for name, shape in CONSTS[FIRST:]:
        sp.dma_start(g[name][:], g["consts"][name]).then_inc(g["rest_loaded"], 16)


def split_weights(nc, dve, g):
    dve.wait_ge(g["rest_loaded"], 16 * (len(CONSTS) - FIRST))
    chain = Chain(dve, g["split"])
    for full, p in ((g["w2"], g["wp"]), (g["b2"], g["bp"])):
        chain.link(nc.vector.tensor_copy(p[0][:, :], full[:, :]))
        chain.link(nc.vector.tensor_tensor(full[:, :], full[:, :], p[0][:, :], ALU.subtract))
        chain.link(nc.vector.tensor_copy(p[1][:, :], full[:, :]))
        chain.link(nc.vector.tensor_tensor(p[2][:, :], full[:, :], p[1][:, :], ALU.subtract))


def stack_weights(sp, g):
    sp.wait_ge(g["split"], 8)
    M = TAPS * C // WQ
    total = 0
    for dst, parts in ((g["wgt_a"], (0, 1, 0)), (g["wgt_b"], (2, 1, 0))):
        for j, p in enumerate(parts):
            for q in range(WQ):
                sp.dma_start(dst[RED * j:RED * (j + 1), q * M:(q + 1) * M],
                             g["wp"][p][RED * q:RED * (q + 1), :]).then_inc(g["stacked"], 16)
                total += 16
    for dst, row, p in ((g["wgt_a"], RP, 0), (g["wgt_b"], RP, 1), (g["wgt_b"], RP + 1, 2)):
        sp.dma_start(dst[row:row + 1, :].rearrange("o (k c) -> o k c", c=C), g["bp"][p][:, :]) \
            .then_inc(g["stacked"], 16)
        total += 16
    sp.wait_ge(g["stacked"], total)


def program(nc, x, consts, out):
    with ExitStack() as ctx:
        g = {name: ctx.enter_context(nc.sbuf_tensor(f"c_{name}", shape, F32)) for name, shape in CONSTS}
        for name, shape in (("bst", [128, B, TILES, 6]), ("mv", [128, B, 2]), ("msq", [128, B]), ("gm", [128, B, 2]),
                            ("var", [128, B]), ("std", [128, B]), ("rstd", [128, B]), ("eps", [128, 1])):
            g[name] = ctx.enter_context(nc.sbuf_tensor(f"n_{name}", shape, F32))
        g["in_x"], g["consts"] = x, consts
        g["x"] = ctx.enter_context(nc.sbuf_tensor("x_map", [128, N], F32))
        g["ps"] = ctx.enter_context(nc.psum_tensor("ps", [128, 8, BANK], F32))
        g.update(semaphores(ctx, nc, "g", "first_loaded rest_loaded split stacked x0_loaded x1_loaded"))
        g["x_loaded"] = [g["x0_loaded"], g["x1_loaded"]]
        g["first_total"] = 16 * FIRST + 1

        with nc.Block() as block:
            @block.gpsimd
            def _(pool):
                nc.gpsimd.memset(g["eps"][:, :], 1e-5).then_inc(g["first_loaded"], 1)

        with ExitStack() as held:
            for name, rows in (("wgt_a", RP + 1), ("wgt_b", RP + 2)):
                g[name] = held.enter_context(nc.sbuf_tensor(name, [rows, TAPS * C], BF16))
            with ExitStack() as parts:
                g["wp"] = [parts.enter_context(nc.sbuf_tensor(f"wp{i}", [WQ * RED, TAPS * C // WQ], BF16))
                           for i in range(3)]
                g["bp"] = [parts.enter_context(nc.sbuf_tensor(f"bp{i}", [TAPS, C], BF16)) for i in range(3)]
                sampling_layer(nc, g, False)
            involution_layer(nc, g)
        sampling_layer(nc, g, True)
        attention_layer(nc, g, out)


def lay_out(i):
    f = np.float32
    pos = np.arange(S).reshape(TILES, 128).T
    tap = np.arange(K2)
    base = np.stack([pos[:, :, None] // W - 1 + tap // 3, pos[:, :, None] % W - 1 + tap % 3], -1)
    w2 = i["L1_conv_w2"].reshape(C, TAPS, RED).transpose(2, 1, 0).reshape(RED, WQ, TAPS * C // WQ)

    def filled(a):
        return np.concatenate([a, np.zeros((RO - len(a),) + a.shape[1:], f)], 0)

    def thrice(b):
        return np.concatenate([filled(b)] * OT, 0)[:, None]

    def rep(a):
        return np.concatenate([a.reshape(RED, -1)] * 3, 0)

    return {
        "ident": np.eye(128, dtype=f),
        "gavg": np.kron(np.eye(C // GROUP, dtype=f), np.full((GROUP, GROUP), 1.0 / GROUP, f)),
        "base": base.reshape(128, -1).astype(f),
        "pw": i["L0_conv_pw_w"].T, "off_w": filled(i["L0_conv_off_w"]).T[:, None, :],
        "off_b": thrice(i["L0_conv_off_b"]),
        "dw": i["L0_conv_dw_w"].reshape(C, K2),
        "w1": rep(i["L1_conv_w1"]).T, "b1": rep(i["L1_conv_b1"]), "gamma": rep(i["L1_conv_gamma"]),
        "beta": rep(i["L1_conv_beta"]),
        "w2": w2.transpose(1, 0, 2).reshape(WQ * RED, -1), "b2": i["L1_conv_b2"].reshape(C, TAPS).T,
        "w_om": filled(i["L2_conv_w_om"].reshape(3 * K2, C, K2)).transpose(1, 2, 0),
        "b_om": thrice(i["L2_conv_b_om"]),
        "w_dc": i["L2_conv_w_dc"].reshape(C, C, K2).transpose(1, 2, 0), "b_dc": i["L2_conv_b_dc"][:, None],
        "wqk": np.stack([i["L3_conv_Wq"].T, i["L3_conv_Wk"].T], 1), "wv": i["L3_conv_Wv"].T,
        "wo": i["L3_conv_Wo"].T,
    }


def kernel(**inputs):
    import concourse.bacc as bacc
    from concourse.bass_utils import run_bass_kernel_spmd

    i = {k: np.asarray(v) for k, v in inputs.items()}
    arrays = {"x": i["x"].reshape(B, C, S)}
    arrays.update(lay_out(i))
    arrays = {k: np.ascontiguousarray(v) for k, v in arrays.items()}
    nc = bacc.Bacc("TRN2", target_bir_lowering=False, num_devices=1)
    aps = {k: nc.dram_tensor(f"in_{k}", v.shape, mybir.dt.from_np(v.dtype), kind="ExternalInput").ap()
           for k, v in arrays.items()}
    out = nc.dram_tensor("out", (B, C, S), F32, kind="ExternalOutput").ap()
    program(nc, aps["x"], aps, out)
    r = run_bass_kernel_spmd(nc, [{f"in_{k}": v for k, v in arrays.items()}], core_ids=[0])
    return r.results[0]["out"].reshape(B, C, H, W)
```
